# Optimizing a Trainium2 kernel written in Bass

```python
import numpy as np
import jax
import jax.numpy as jnp

def _softmax(x, axis=-1):
    return jax.nn.softmax(x, axis=axis)

def _gelu(x):
    return jax.nn.gelu(x, approximate=True)

def _silu(x):
    return jax.nn.silu(x)

def _sigmoid(x):
    return jax.nn.sigmoid(x)

def _layernorm(x, axis=-1, eps=1e-05):
    m = jnp.mean(x, axis=axis, keepdims=True)
    v = jnp.var(x, axis=axis, keepdims=True)
    return (x - m) / jnp.sqrt(v + eps)

def _scatter_add(tgt, idx, src, axis=0):
    return tgt.at[idx].add(src)

def _segment_sum(src, seg, n):
    return jax.ops.segment_sum(src, seg, n)
kernel_name = 'mk_seq_postln_d1_jaxref_r8_8416f4'

def setup_inputs(seed: int=0):
    np.random.seed(seed)
    _w = jnp.asarray

    def _L0_attn_setup():
        import jax, jax.numpy as jnp
        import numpy as np
        INFTY_APPROX = 1e+30
        ROTARY_BASE = 10000.0
        D_HEAD = 128

        def rope(x, base=ROTARY_BASE):
            *_, length, width = x.shape
            half = width // 2
            positions = jnp.arange(length)[:, None].astype(jnp.float32)
            ang_freqs = jnp.power(base, -jnp.arange(half) / half)[None, :]
            radians = positions * ang_freqs
            cos = jnp.cos(radians).astype(x.dtype)[None, None]
            sin = jnp.sin(radians).astype(x.dtype)[None, None]
            even, odd = jnp.split(x, 2, axis=-1)
            return jnp.concatenate([even * cos - odd * sin, even * sin + odd * cos], axis=-1)
        key = jax.random.key(seed)
        ks = jax.random.split(key, 5)
        B, T, M, H, D = (2, 256, 128, 8, D_HEAD)
        x = jax.random.normal(ks[0], (B, T, M), dtype=jnp.float32)
        scale = M ** (-0.5)
        wq = jax.random.normal(ks[1], (M, H, D), dtype=jnp.float32) * scale
        wk = jax.random.normal(ks[2], (M, H, D), dtype=jnp.float32) * scale
        wv = jax.random.normal(ks[3], (M, H, D), dtype=jnp.float32) * scale
        wo = jax.random.normal(ks[4], (H, D, M), dtype=jnp.float32) * scale
        return {'x': x, 'wq': wq, 'wk': wk, 'wv': wv, 'wo': wo}
    _L0_attn_in = _L0_attn_setup()

    def _L0_ffn_setup():
        import jax, jax.numpy as jnp
        import numpy as np
        EPS = 1e-12

        def rms_norm(t, gamma):
            n = jnp.maximum(jnp.linalg.norm(t, axis=-1, keepdims=True), EPS)
            scale = jnp.sqrt(jnp.asarray(t.shape[-1], t.dtype))
            return t / n * scale * gamma
        key = jax.random.key(seed)
        ks = jax.random.split(key, 4)
        b, s, d = (4, 512, 128)
        e, t = (8, 64)
        hidden = 4 * d
        return {'x': jax.random.normal(ks[0], (b, s, d), dtype=jnp.float32), 'gamma_x': jnp.ones((d,), dtype=jnp.float32), 'gamma_slot': jnp.ones((d,), dtype=jnp.float32), 'slot_embeds': jax.random.normal(ks[1], (e, t, d), dtype=jnp.float32), 'w1': jax.random.normal(ks[2], (d, hidden), dtype=jnp.float32) * (1.0 / np.sqrt(d)), 'w2': jax.random.normal(ks[3], (hidden, d), dtype=jnp.float32) * (1.0 / np.sqrt(hidden))}
    _L0_ffn_in = _L0_ffn_setup()
    _d = {'L0_attn_x': _L0_attn_in['x'], 'L0_attn_wq': _L0_attn_in['wq'], 'L0_attn_wk': _L0_attn_in['wk'], 'L0_attn_wv': _L0_attn_in['wv'], 'L0_attn_wo': _L0_attn_in['wo'], 'L0_ffn_gamma_x': _L0_ffn_in['gamma_x'], 'L0_ffn_gamma_slot': _L0_ffn_in['gamma_slot'], 'L0_ffn_slot_embeds': _L0_ffn_in['slot_embeds'], 'L0_ffn_w1': _L0_ffn_in['w1'], 'L0_ffn_w2': _L0_ffn_in['w2']}
    _x0 = _d['L0_attn_x']
    _d['L0_attn_x'] = jax.random.normal(jax.random.fold_in(jax.random.key(seed), 1), (8, 1024, 128), dtype=_x0.dtype)
    del _x0
    return _d

def reference(L0_attn_x, L0_attn_wq, L0_attn_wk, L0_attn_wv, L0_attn_wo, L0_ffn_gamma_x, L0_ffn_gamma_slot, L0_ffn_slot_embeds, L0_ffn_w1, L0_ffn_w2):

    def _L0_attn_ref(x, wq, wk, wv, wo):
        import jax, jax.numpy as jnp
        import numpy as np
        INFTY_APPROX = 1e+30
        ROTARY_BASE = 10000.0
        D_HEAD = 128

        def rope(x, base=ROTARY_BASE):
            *_, length, width = x.shape
            half = width // 2
            positions = jnp.arange(length)[:, None].astype(jnp.float32)
            ang_freqs = jnp.power(base, -jnp.arange(half) / half)[None, :]
            radians = positions * ang_freqs
            cos = jnp.cos(radians).astype(x.dtype)[None, None]
            sin = jnp.sin(radians).astype(x.dtype)[None, None]
            even, odd = jnp.split(x, 2, axis=-1)
            return jnp.concatenate([even * cos - odd * sin, even * sin + odd * cos], axis=-1)
        B, T, M = x.shape
        q = jnp.einsum('bim,mhd->bhid', x, wq)
        k = jnp.einsum('bim,mhd->bhid', x, wk)
        v = jnp.einsum('bim,mhd->bhid', x, wv)
        q = rope(q)
        k = rope(k)
        s = jnp.einsum('bhid,bhjd->bhij', q, k) / jnp.asarray(D_HEAD, q.dtype)
        i = jnp.arange(T)[:, None]
        j = jnp.arange(T)[None, :]
        mask = (i < j)[None, None]
        s = s - jnp.asarray(INFTY_APPROX, s.dtype) * mask
        p = jax.nn.softmax(s, axis=-1)
        o = jnp.einsum('bhij,bhjd->bhid', p, v)
        return jnp.einsum('bhid,hdm->bim', o, wo)

    def _L0_ffn_ref(x, gamma_x, gamma_slot, slot_embeds, w1, w2):
        import jax, jax.numpy as jnp
        import numpy as np
        EPS = 1e-12

        def rms_norm(t, gamma):
            n = jnp.maximum(jnp.linalg.norm(t, axis=-1, keepdims=True), EPS)
            scale = jnp.sqrt(jnp.asarray(t.shape[-1], t.dtype))
            return t / n * scale * gamma
        b, s, d = x.shape
        e, t, _ = slot_embeds.shape
        xn = rms_norm(x, gamma_x)
        se = rms_norm(slot_embeds, gamma_slot)
        logits = jnp.einsum('bsd,etd->bset', xn, se)
        dispatch = jax.nn.softmax(logits, axis=1)
        slots = jnp.einsum('bsd,bset->betd', xn, dispatch)
        h = jax.nn.gelu(slots @ w1, approximate=False)
        processed = h @ w2
        combine = jax.nn.softmax(logits.reshape(b, s, e * t), axis=-1)
        out = jnp.einsum('bnd,bsn->bsd', processed.reshape(b, e * t, d), combine)
        return out
    x = L0_attn_x
    x = _layernorm(x + _L0_attn_ref(x, L0_attn_wq, L0_attn_wk, L0_attn_wv, L0_attn_wo), axis=-1)
    x = _layernorm(x + _L0_ffn_ref(x, L0_ffn_gamma_x, L0_ffn_gamma_slot, L0_ffn_slot_embeds, L0_ffn_w1, L0_ffn_w2), axis=-1)
    return x

_drawn_inputs = setup_inputs


def setup_inputs(seed=0):
    import zlib

    import numpy as np

    out = dict(_drawn_inputs(seed))
    spreads = {'L0_ffn_gamma_x': (1.0, 0.2), 'L0_ffn_gamma_slot': (1.0, 0.2)}
    factors = {}
    for name, (base, spread) in spreads.items():
        noise = np.random.default_rng([zlib.crc32(name.encode()), seed]).standard_normal(out[name].shape)
        drawn = base * np.exp(spread * noise) if base else spread * noise
        out[name] = jnp.asarray(drawn.astype(out[name].dtype))
    for name, factor in factors.items():
        out[name] = (out[name] * factor).astype(out[name].dtype)
    return out
```

```python
from contextlib import ExitStack

import numpy as np

import concourse.bass as bass
from concourse import mybir

P = 128
BANK = 512
ALU = mybir.AluOpType
ACT = mybir.ActivationFunctionType
AX = mybir.AxisListType
F32 = mybir.dt.float32
F32R = mybir.dt.float32r
BF16 = mybir.dt.bfloat16
ROTARY_BASE = 10000.0
MASKED = -1e30
LN_EPS = 1e-5

WQ_HI, WQ_LO, WK_HI, WK_LO, WVO_HI, WVO_LO = range(6)


class Scope:

    def __init__(self, nc, ctx):
        self.nc, self.ctx = nc, ctx

    def sb(self, name, shape, dt):
        return self.ctx.enter_context(self.nc.sbuf_tensor(name, shape, dt))

    def ps(self, name, shape):
        return self.ctx.enter_context(self.nc.psum_tensor(name, shape, F32))

    def sem(self, name):
        return self.ctx.enter_context(self.nc.semaphore(name))


def matmul_split(pe, out, stat_hi, stat_lo, mov_hi, mov_lo, start, stop):
    pe.matmul(out, stat_hi, mov_hi, start=start, stop=False, skip_group_check=True)
    pe.matmul(out, stat_hi, mov_lo, start=False, stop=False, skip_group_check=True)
    return pe.matmul(out, stat_lo, mov_hi, start=False, stop=stop, skip_group_check=True)


def wait_apart(eng, sem, value, ticks):
    eng.wait_ge(sem, value)
    eng.sem_inc(ticks, 1)


def f32(ap):
    return ap.bitcast(F32)


def prepare_block(nc, x, wq, wk, wv, wo, w_split, x_split):
    B, T, M = x.shape
    H = wq.shape[1]
    NT = T // P
    with ExitStack() as ctx:
        s = Scope(nc, ctx)
        w_raw = s.sb("w_raw", [P, 4, H * P], F32)
        wv_t = s.sb("wv_t", [P, H, P], F32)
        w_out = s.sb("w_out", [P, H, 6, P], F32R)
        x_row = s.sb("x_row", [P, 2, NT, M], F32)
        x_out = s.sb("x_out", [P, 2, 2, T], F32R)
        ident = s.sb("ident0", [P, P], F32)
        ps_w = s.ps("ps_w", [P, 2, H * P])
        ps_x = s.ps("ps_x", [P, 2, T])
        ident_made = s.sem("ident_made0")
        w_landed = s.sem("w_landed")
        qk_split = s.sem("qk_split")
        wv_turned, wv_copied = s.sem("wv_turned"), s.sem("wv_copied")
        wvo_made, wvo_copied, wvo_split = s.sem("wvo_made"), s.sem("wvo_copied"), s.sem("wvo_split")
        x_landed = [s.sem(f"x_landed{i}") for i in range(2)]
        x_turned, x_hi, x_lo = s.sem("x_turned"), s.sem("x_hi"), s.sem("x_lo")
        x_stored = [s.sem(f"x_stored{i}") for i in range(2)]
        w_stored = s.sem("w_stored")

        block = ctx.enter_context(nc.Block())

        @block.sync
        def _(sp):
            for i, w in enumerate((wq, wk, wv)):
                sp.dma_start(w_raw[:, i, :], w.rearrange("m h d -> m (h d)")).then_inc(w_landed, 16)
            sp.dma_start(w_raw[:, 3, :].rearrange("p (h m) -> p h m", h=H),
                         wo.rearrange("h d m -> d h m")).then_inc(w_landed, 16)
            sp.wait_ge(qk_split, 4)
            sp.wait_ge(wvo_split, 1)
            sp.dma_start(w_split.rearrange("h m s d -> m h s d"), f32(w_out[:, :, :, :])).then_inc(w_stored, 16)
            sp.wait_ge(w_stored, 16)

        @block.gpsimd
        def _(pool):
            pool.memset(ident[:, :], 0.0).then_inc(ident_made, 1)
            pool.wait_ge(ident_made, 1)
            pool.affine_select(out=ident[:, :], in_=ident[:, :], compare_op=ALU.not_equal, fill=1.0,
                               base=0, pattern=[[-1, P]], channel_multiplier=1).then_inc(ident_made, 1)

        @block.scalar
        def _(act):
            def load(b):
                act.dma_start(x_row[:, b % 2, :, :],
                              x[b, :, :].rearrange("(t p) m -> p t m", p=P)).then_inc(x_landed[b % 2], 16)

            load(0)
            load(1)
            act.wait_ge(wv_turned, 1)
            act.activation(wv_t[:, :, :], ps_w[:, 0, :].rearrange("p (h m) -> p h m", h=H),
                           ACT.Copy).then_inc(wv_copied, 1)
            for b in range(B):
                act.wait_ge(x_turned, b + 1)
                if b + 2 < B:
                    load(b + 2)
                if b >= 2:
                    act.wait_ge(x_stored[b % 2], 16 * (b // 2))
                act.activation(x_out[:, b % 2, 0, :], ps_x[:, b % 2, :], ACT.Copy).then_inc(x_hi, 1)
                act.wait_ge(x_lo, b + 1)
                act.dma_start(x_split[b, :, :, :], f32(x_out[:, b % 2, :, :])).then_inc(x_stored[b % 2], 16)
                if b == B - 1:
                    act.dma_start(x_split[B, :, :, :], f32(x_out[:, b % 2, :, :])).then_inc(x_stored[b % 2], 16)
            act.wait_ge(x_stored[0], 16 * (B // 2))
            act.wait_ge(x_stored[1], 16 * (B // 2 + 1))

        @block.vector
        def _(dve):
            dve.wait_ge(w_landed, 64)
            for i, (hi, lo, scale) in enumerate(((WQ_HI, WQ_LO, 1.0 / P), (WK_HI, WK_LO, 1.0))):
                raw = w_raw[:, i, :].rearrange("p (h d) -> p h d", h=H)
                dve.tensor_scalar(w_out[:, :, hi, :], raw, scale, None, ALU.mult).then_inc(qk_split, 1)
                dve.wait_ge(qk_split, 2 * i + 1)
                dve.scalar_tensor_tensor(w_out[:, :, lo, :], raw, scale, f32(w_out[:, :, hi, :]),
                                         ALU.mult, ALU.subtract).then_inc(qk_split, 1)
            dve.wait_ge(wvo_made, 1)
            made = ps_w[:, 1, :].rearrange("p (h m) -> p h m", h=H)
            dve.tensor_copy(w_out[:, :, WVO_HI, :], made).then_inc(wvo_copied, 1)
            dve.wait_ge(wvo_copied, 1)
            dve.tensor_tensor(w_out[:, :, WVO_LO, :], made, f32(w_out[:, :, WVO_HI, :]),
                              ALU.subtract).then_inc(wvo_split, 1)
            for b in range(B):
                dve.wait_ge(x_hi, b + 1)
                dve.tensor_tensor(x_out[:, b % 2, 1, :], ps_x[:, b % 2, :], f32(x_out[:, b % 2, 0, :]),
                                  ALU.subtract).then_inc(x_lo, 1)

        @block.tensor
        def _(pe):
            pe.wait_ge(ident_made, 2)
            pe.wait_ge(w_landed, 64)
            for h in range(H):
                last = pe.transpose(ps_w[:, 0, h * P:(h + 1) * P], w_raw[:, 2, h * P:(h + 1) * P], ident[:, :])
            last.then_inc(wv_turned, 1)
            pe.wait_ge(wv_copied, 1)
            for h in range(H):
                last = pe.matmul(ps_w[:, 1, h * P:(h + 1) * P], wv_t[:, h, :],
                                 w_raw[:, 3, h * P:(h + 1) * P], start=True, stop=True)
            last.then_inc(wvo_made, 1)
            for b in range(B):
                pe.wait_ge(x_landed[b % 2], 16 * (b // 2 + 1))
                if b >= 2:
                    pe.wait_ge(x_lo, b - 1)
                for t in range(NT):
                    last = pe.transpose(ps_x[:, b % 2, t * P:(t + 1) * P], x_row[:, b % 2, t, :], ident[:, :])
                last.then_inc(x_turned, 1)


def rope_tables(T, D):
    half = D // 2
    freq = np.power(np.float32(ROTARY_BASE), -np.arange(half, dtype=np.float32) / np.float32(half))
    ang = (np.arange(T, dtype=np.float32)[:, None] * freq.astype(np.float32)[None, :]).T
    cos, sin = np.cos(ang).astype(np.float32), np.sin(ang).astype(np.float32)
    return np.concatenate([cos, cos]), np.concatenate([-sin, sin])


SLOT_TILES = ((7,), (6,), (5,), (4,), (3, 2), (1, 0))
TILES = (7, 6, 5, 4, 3, 2, 1, 0)
TURN_BANKS = tuple(
    [(s, [(t, 0, 4)]) if half == 0 else (s, [(t, 4, t + 1)])
     for s, t in enumerate((7, 6, 5, 4)) for half in range(2)]
    + [(4, [(3, 0, 4)]), (4, [(2, 0, 3)]), (5, [(1, 0, 2), (0, 0, 1)])])
NB_TURN = len(TURN_BANKS)
BANKS_G1 = 8
FILLS = 9


def attention_block(nc, w_split, x_split, rope_c, rope_s, y_t, B, H, T):
    NT = T // P
    D = P
    assert NT == 8 and H % 2 == 0
    width = {t: P * (t + 1) for t in TILES}
    p_at, at = {}, 0
    for t in TILES:
        p_at[t] = at
        at += width[t]
    stat_col = {t: i for i, t in enumerate(TILES)}

    with ExitStack() as ctx:
        s = Scope(nc, ctx)
        rope = s.sb("rope", [P, 2, T], F32)
        w_in = [s.sb(f"w_in{i}", [P, 6, D], F32R) for i in range(2)]
        x_in = [s.sb(f"x_in{i}", [P, 2, T], F32R) for i in range(2)]
        qk = [[s.sb(f"{n}{i}", [P, 2, T], F32R) for n in "qk"] for i in range(2)]
        v_in = [s.sb(f"v{i}", [P, 2, T], F32R) for i in range(2)]
        unrot = [s.sb(f"unrot_{n}", [P, T], F32) for n in "qk"]
        swapped = [s.sb(f"swapped_{n}", [P, T], F32) for n in "qk"]
        probs = s.sb("probs", [P, at], F32)
        pt = [s.sb("pt_low", [P, 2, 4, BANK], F32R), s.sb("pt_high", [P, 2, 8, BANK], F32R)]
        y_out = s.sb("y_out", [P, T], F32)
        neg_max = s.sb("neg_max", [P, 2, NT], F32)
        sums = s.sb("sums", [P, 2, NT], F32)
        inv = s.sb("inv", [P, 2, NT], F32)
        ident = s.sb("ident1", [P, P], F32)
        ident_b = s.sb("ident_b", [P, P], BF16)
        mask_b = s.sb("mask_b", [P, P], BF16)
        zeros_b = s.sb("zeros_b", [P, BANK], BF16)
        ps_slot = s.ps("ps_slot", [P, 2, T])
        ps_turn = s.ps("ps_turn", [P, 2, BANK])
        ps_y = s.ps("ps_y", [P, 2, BANK])

        consts, ticks = s.sem("consts"), s.sem("ticks")
        rope_landed = s.sem("rope_landed")
        in_landed = [s.sem(f"in_landed{i}") for i in range(2)]
        filled = s.sem("filled")
        turned = s.sem("turned")
        y_zeroed = s.sem("y_zeroed")
        pv_done = s.sem("pv_done")
        maxed = s.sem("maxed")
        inverted = s.sem("inverted")
        v_lo, rot_mul, qk_lo, turn_lo = s.sem("v_lo"), s.sem("rot_mul"), s.sem("qk_lo"), s.sem("turn_lo")
        exped = s.sem("exped")
        v_hi, qk_raw, qk_hi, turn_hi = s.sem("v_hi"), s.sem("qk_raw"), s.sem("qk_hi"), s.sem("turn_hi")
        y_copied, y_free = s.sem("y_copied"), s.sem("y_free")
        normed = s.sem("normed")
        rot_sum = s.sem("rot_sum")
        swap_landed = [s.sem(f"swap_landed_{n}") for n in "qk"]

        F_S7, F_S6, F_V, F_S5, F_Q, F_S4, F_K, F_S32, F_S10 = range(3, 12)

        def slot(fill, par):
            return ps_slot[:, (fill + par * FILLS - 1) % 2, :]

        def turn_views(bank_no, par, part):
            at = 0
            bank = (bank_no + par * NB_TURN) % 2
            for t, j0, j1 in TURN_BANKS[bank_no][1]:
                c = (t % 4) * P
                src = ps_turn[:, bank, at:at + (j1 - j0) * P].rearrange("p (j c) -> p j c", c=P)
                yield pt[t // 4][:, part, j0:j1, c:c + P], src
                at += (j1 - j0) * P

        block = ctx.enter_context(nc.Block())

        @block.sync
        def _(sp):
            sp.dma_start(rope[:, 0, :], rope_c).then_inc(rope_landed, 16)
            sp.dma_start(rope[:, 1, :], rope_s).then_inc(rope_landed, 16)

            def load(w_head, x_batch, par):
                sp.dma_start(f32(w_in[par][:, :, :]), w_split[w_head, :, :, :]).then_inc(in_landed[par], 16)
                sp.dma_start(f32(x_in[par][:, :, :]), x_split[x_batch, :, :, :]).then_inc(in_landed[par], 16)

            def swap(which, raw_count):
                sp.wait_ge(qk_raw, raw_count)
                for half in range(2):
                    sp.dma_start(swapped[which][64 * half:64 * half + 64, :],
                                 unrot[which][64 - 64 * half:128 - 64 * half, :]).then_inc(swap_landed[which], 16)

            load(0, 0, 0)
            load(1, 0, 1)
            swap(0, 1)
            swap(1, 2)

            def head(head_no, par, next_w, next_x):
                sp.wait_ge(filled, head_no * FILLS + F_V)
                load(next_w, next_x, par)
                swap(0, head_no * 2 + 3)
                swap(1, head_no * 2 + 4)

            with sp.Fori(0, B) as b:
                with sp.Fori(0, H // 2 - 1) as pair:
                    for par in range(2):
                        head(b * H + pair * 2 + par, par, pair * 2 + 2 + par, b)
                for par in range(2):
                    head(b * H + (H - 2 + par), par, par, b + 1)
                sp.wait_ge(y_copied, b + 1)
                sp.dma_start(y_t[b, :, :], y_out[:, :]).then_inc(y_free, 16)
            sp.wait_ge(y_free, 16 * B + 1)
            for par in range(2):
                sp.wait_ge(in_landed[par], 32 * (B * H // 2 + 1))

        @block.gpsimd
        def _(pool):
            pool.memset(ident[:, :], 0.0).then_inc(consts, 1)
            pool.memset(ident_b[:, :], 0.0).then_inc(consts, 1)
            pool.memset(mask_b[:, :], 0.0).then_inc(consts, 1)
            pool.memset(zeros_b[:, :], 0.0).then_inc(consts, 1)
            pool.memset(y_out[:, :], 0.0).then_inc(y_free, 1)
            pool.wait_ge(consts, 4)
            for m in (ident, ident_b):
                pool.affine_select(out=m[:, :], in_=m[:, :], compare_op=ALU.not_equal, fill=1.0,
                                   base=0, pattern=[[-1, P]], channel_multiplier=1).then_inc(consts, 1)
            pool.affine_select(out=mask_b[:, :], in_=mask_b[:, :], compare_op=ALU.is_ge, fill=MASKED,
                               base=0, pattern=[[-1, P]], channel_multiplier=1).then_inc(consts, 1)

            def rotate(which, count):
                pool.wait_ge(rot_mul, count * 2)
                pool.tensor_tensor(unrot[which][:, :], unrot[which][:, :], swapped[which][:, :],
                                   ALU.add).then_inc(rot_sum, 1)

            def norm(head_no, par, slot_no):
                wait_apart(pool, inverted, head_no * 6 + slot_no + 1, ticks)
                for t in SLOT_TILES[slot_no]:
                    tile = probs[:, p_at[t]:p_at[t] + width[t]]
                    pool.tensor_scalar(tile, tile, inv[:, par, stat_col[t]:stat_col[t] + 1], 1.0,
                                       ALU.mult, ALU.mult).then_inc(normed, 1)

            rotate(0, 1)
            rotate(1, 2)

            def head(head_no, par):
                norm(head_no, par, 0)
                norm(head_no, par, 1)
                norm(head_no, par, 2)
                norm(head_no, par, 3)
                rotate(0, head_no * 2 + 3)
                norm(head_no, par, 4)
                norm(head_no, par, 5)
                rotate(1, head_no * 2 + 4)

            with pool.Fori(0, B) as b:
                with pool.Fori(0, H // 2) as pair:
                    for par in range(2):
                        head(b * H + pair * 2 + par, par)

        @block.scalar
        def _(act):
            def exp(head_no, par, slot_no):
                fill = (F_S7, F_S6, F_S5, F_S4, F_S32, F_S10)[slot_no]
                for i, t in enumerate(SLOT_TILES[slot_no]):
                    c = stat_col[t]
                    act.wait_ge(maxed, head_no * NT + c + 1)
                    src = slot(fill, par)[:, i * BANK:i * BANK + width[t]]
                    last = act.activation(probs[:, p_at[t]:p_at[t] + width[t]], src, ACT.Exp,
                                          bias=neg_max[:, par, c:c + 1], accum_out=sums[:, par, c:c + 1])
                last.then_inc(exped, 1)

            def raw(which, fill_no, par, fill, count):
                act.wait_ge(filled, fill_no)
                if count is not None:
                    act.wait_ge(qk_lo, count)
                act.activation(unrot[which][:, :], slot(fill, par), ACT.Copy).then_inc(qk_raw, 1)

            def split_hi(which, par, count):
                act.wait_ge(rot_sum, count)
                act.activation(qk[par][which][:, 0, :], unrot[which][:, :], ACT.Copy).then_inc(qk_hi, 1)

            def v_split_hi(head_no, par):
                act.wait_ge(filled, head_no * FILLS + F_V)
                for h in range(2):
                    cols = slice(h * BANK, (h + 1) * BANK)
                    act.activation(v_in[par][:, 0, cols], slot(F_V, par)[:, cols], ACT.Copy).then_inc(v_hi, 1)

            def turn_split_hi(head_no, par, bank_no):
                act.wait_ge(turned, head_no * NB_TURN + bank_no + 1)
                for dst, src in turn_views(bank_no, par, 0):
                    last = act.activation(dst, src, ACT.Copy)
                last.then_inc(turn_hi, 1)

            raw(0, 1, 0, 1, None)
            raw(1, 2, 0, 2, None)
            split_hi(0, 0, 1)
            split_hi(1, 0, 2)

            def head(head_no, par):
                nxt = 1 - par
                exp(head_no, par, 0)
                exp(head_no, par, 1)
                v_split_hi(head_no, par)
                turn_split_hi(head_no, par, 0)
                turn_split_hi(head_no, par, 1)
                exp(head_no, par, 2)
                turn_split_hi(head_no, par, 2)
                turn_split_hi(head_no, par, 3)
                raw(0, head_no * FILLS + F_Q, par, F_Q, head_no * 2 + 1)
                turn_split_hi(head_no, par, 4)
                turn_split_hi(head_no, par, 5)
                exp(head_no, par, 3)
                raw(1, head_no * FILLS + F_K, par, F_K, head_no * 2 + 2)
                turn_split_hi(head_no, par, 6)
                turn_split_hi(head_no, par, 7)
                exp(head_no, par, 4)
                exp(head_no, par, 5)
                split_hi(0, nxt, head_no * 2 + 3)
                turn_split_hi(head_no, par, 8)
                turn_split_hi(head_no, par, 9)
                turn_split_hi(head_no, par, 10)
                split_hi(1, nxt, head_no * 2 + 4)

            with act.Fori(0, B) as b:
                with act.Fori(0, H // 2) as pair:
                    for par in range(2):
                        head(b * H + pair * 2 + par, par)
                act.wait_ge(pv_done, b * H + H)
                act.wait_ge(y_free, b * 16 + 1)
                act.activation(y_out[:, :].rearrange("p (g c) -> p g c", g=2), ps_y[:, :, :],
                               ACT.Copy).then_inc(y_copied, 1)
            exp(B * H, 0, 0)

        @block.vector
        def _(dve):
            dve.wait_ge(rope_landed, 32)

            def rowmax(head_no, par, slot_no):
                fill = (F_S7, F_S6, F_S5, F_S4, F_S32, F_S10)[slot_no]
                dve.wait_ge(filled, head_no * FILLS + fill)
                for i, t in enumerate(SLOT_TILES[slot_no]):
                    c = stat_col[t]
                    dve.tensor_reduce(neg_max[:, par, c:c + 1], slot(fill, par)[:, i * BANK:i * BANK + width[t]],
                                      AX.X, ALU.max, negate=True).then_inc(maxed, 1)

            def invert(head_no, par, slot_no):
                dve.wait_ge(exped, head_no * 6 + slot_no + 1)
                c = stat_col[SLOT_TILES[slot_no][0]]
                n = len(SLOT_TILES[slot_no])
                dve.reciprocal(inv[:, par, c:c + n], sums[:, par, c:c + n]).then_inc(inverted, 1)

            def rotate_mul_first(which, count):
                dve.wait_ge(swap_landed[which], count * 32)
                dve.tensor_tensor(unrot[which][:, :], unrot[which][:, :], rope[:, 0, :], ALU.mult).then_inc(rot_mul, 1)

            def rotate_mul_second(which):
                dve.tensor_tensor(swapped[which][:, :], swapped[which][:, :], rope[:, 1, :],
                                  ALU.mult).then_inc(rot_mul, 1)

            def split_lo(which, par, count):
                dve.wait_ge(qk_hi, count)
                dve.tensor_tensor(qk[par][which][:, 1, :], unrot[which][:, :], f32(qk[par][which][:, 0, :]),
                                  ALU.subtract).then_inc(qk_lo, 1)

            def v_split_lo(head_no, par):
                for h in range(2):
                    dve.wait_ge(v_hi, head_no * 2 + h + 1)
                    cols = slice(h * BANK, (h + 1) * BANK)
                    dve.tensor_tensor(v_in[par][:, 1, cols], slot(F_V, par)[:, cols], f32(v_in[par][:, 0, cols]),
                                      ALU.subtract).then_inc(v_lo, 1)

            def turn_split_lo(head_no, par, bank_no):
                dve.wait_ge(turn_hi, head_no * NB_TURN + bank_no + 1)
                for (dst, src), (hi, _) in zip(turn_views(bank_no, par, 1), turn_views(bank_no, par, 0)):
                    last = dve.tensor_tensor(dst, src, f32(hi), ALU.subtract)
                last.then_inc(turn_lo, 1)

            for par in range(2):
                dve.memset(inv[:, par, :], 0.0).then_inc(turn_lo, 1)
            dve.wait_ge(turn_lo, 2)
            for which in range(2):
                rotate_mul_first(which, 1)
                rotate_mul_second(which)
            split_lo(0, 0, 1)
            split_lo(1, 0, 2)

            def head(head_no, par):
                nxt = 1 - par
                rowmax(head_no, par, 0)
                rowmax(head_no, par, 1)
                invert(head_no, par, 0)
                invert(head_no, par, 1)
                v_split_lo(head_no, par)
                turn_split_lo(head_no, par, 0)
                turn_split_lo(head_no, par, 1)
                rowmax(head_no, par, 2)
                turn_split_lo(head_no, par, 2)
                invert(head_no, par, 2)
                turn_split_lo(head_no, par, 3)
                turn_split_lo(head_no, par, 4)
                turn_split_lo(head_no, par, 5)
                rowmax(head_no, par, 3)
                rotate_mul_first(0, head_no + 2)
                invert(head_no, par, 3)
                rotate_mul_second(0)
                turn_split_lo(head_no, par, 6)
                turn_split_lo(head_no, par, 7)
                rowmax(head_no, par, 4)
                rowmax(head_no, par, 5)
                invert(head_no, par, 4)
                rotate_mul_first(1, head_no + 2)
                invert(head_no, par, 5)
                rotate_mul_second(1)
                split_lo(0, nxt, head_no * 2 + 3)
                turn_split_lo(head_no, par, 8)
                turn_split_lo(head_no, par, 9)
                turn_split_lo(head_no, par, 10)
                split_lo(1, nxt, head_no * 2 + 4)

            with dve.Fori(0, B) as b:
                with dve.Fori(0, H // 2) as pair:
                    for par in range(2):
                        head(b * H + pair * 2 + par, par)
            rowmax(B * H, 0, 0)

        @block.tensor
        def _(pe):
            pe.wait_ge(consts, 7)

            def project(which, w_par, in_count, fill, par, free_sem, free_count):
                pe.wait_ge(in_landed[w_par], in_count)
                if free_sem is not None:
                    pe.wait_ge(free_sem, free_count)
                hi, lo = ((WQ_HI, WQ_LO), (WK_HI, WK_LO))[which]
                for c in range(2):
                    cols = slice(c * BANK, (c + 1) * BANK)
                    last = matmul_split(pe, slot(fill, par)[:, cols], w_in[w_par][:, hi, :], w_in[w_par][:, lo, :],
                                        x_in[w_par][:, 0, cols], x_in[w_par][:, 1, cols], True, True)
                last.then_inc(filled, 1)

            def project_v(w_par, fill, par, free_count):
                pe.wait_ge(exped, free_count)
                for t in range(NT):
                    cols = slice(t * P, (t + 1) * P)
                    last = matmul_split(pe, slot(fill, par)[:, cols], x_in[w_par][:, 0, cols], x_in[w_par][:, 1, cols],
                                        w_in[w_par][:, WVO_HI, :], w_in[w_par][:, WVO_LO, :], True, True)
                last.then_inc(filled, 1)

            def scores(of_par, tiles, fill, par):
                q, k = qk[of_par]
                for i, t in enumerate(tiles):
                    rows = slice(t * P, (t + 1) * P)
                    for c0 in range(0, width[t], BANK):
                        n = min(BANK, width[t] - c0)
                        out = slot(fill, par)[:, i * BANK + c0:i * BANK + c0 + n]
                        pe.matmul(out, q[:, 0, rows], k[:, 0, c0:c0 + n], start=True, stop=False,
                                  skip_group_check=True)
                        if c0 + n == width[t]:
                            pe.matmul(out[:, n - P:n], ident_b[:, :], mask_b[:, :], start=False, stop=False,
                                      skip_group_check=True)
                        pe.matmul(out, q[:, 0, rows], k[:, 1, c0:c0 + n], start=False, stop=False,
                                  skip_group_check=True)
                        last = pe.matmul(out, q[:, 1, rows], k[:, 0, c0:c0 + n], start=False, stop=True,
                                         skip_group_check=True)
                last.then_inc(filled, 1)

            def turn(head_no, par, slot_no):
                c = max(stat_col[t] for t in SLOT_TILES[slot_no])
                pe.wait_ge(normed, head_no * NT + c + 1)
                for bank_no, (from_slot, parts) in enumerate(TURN_BANKS):
                    if from_slot != slot_no:
                        continue
                    pe.wait_ge(turn_lo, head_no * NB_TURN + bank_no + 1)
                    bank, at = (bank_no + par * NB_TURN) % 2, 0
                    for t, j0, j1 in parts:
                        for j in range(j0, j1):
                            last = pe.transpose(ps_turn[:, bank, at:at + P],
                                                probs[:, p_at[t] + j * P:p_at[t] + (j + 1) * P], ident[:, :])
                            at += P
                    last.then_inc(turned, 1)

            def weigh(par, g):
                for j in range(4 * g + 4):
                    c0 = max(0, j - 4 * g) * P
                    keys = slice(j * P, (j + 1) * P)
                    last = matmul_split(pe, ps_y[:, g, c0:BANK], v_in[par][:, 0, keys], v_in[par][:, 1, keys],
                                        pt[g][:, 0, j, c0:BANK], pt[g][:, 1, j, c0:BANK], False, False)
                return last

            def zero_y():
                for g in range(2):
                    pe.matmul(ps_y[:, g, :], zeros_b[:, 0:P], zeros_b[:, :], start=True, stop=False,
                              skip_group_check=True)

            project(0, 0, 32, 1, 0, None, 0)
            project(1, 0, 32, 2, 0, None, 0)
            pe.wait_ge(qk_lo, 2)
            scores(0, (7,), F_S7, 0)
            scores(0, (6,), F_S6, 0)
            project_v(0, F_V, 0, 1)
            zero_y()

            def head(head_no, par, next_in):
                nxt = 1 - par
                turn(head_no, par, 0)
                pe.wait_ge(exped, head_no * 6 + 2)
                scores(par, (5,), F_S5, par)
                turn(head_no, par, 1)
                project(0, nxt, next_in, F_Q, par, v_lo, head_no * 2 + 2)
                turn(head_no, par, 2)
                pe.wait_ge(exped, head_no * 6 + 3)
                scores(par, (4,), F_S4, par)
                project(1, nxt, next_in, F_K, par, qk_raw, head_no * 2 + 3)
                turn(head_no, par, 3)
                pe.wait_ge(exped, head_no * 6 + 4)
                scores(par, (3, 2), F_S32, par)
                pe.wait_ge(qk_raw, head_no * 2 + 4)
                scores(par, (1, 0), F_S10, par)
                pe.wait_ge(turn_lo, head_no * NB_TURN + 2 + BANKS_G1)
                weigh(par, 1)
                turn(head_no, par, 4)
                turn(head_no, par, 5)
                pe.wait_ge(qk_lo, head_no * 2 + 4)
                pe.wait_ge(exped, head_no * 6 + 5)
                scores(nxt, (7,), F_S10 + 1, par)
                pe.wait_ge(exped, head_no * 6 + 6)
                scores(nxt, (6,), F_S10 + 2, par)
                pe.wait_ge(turn_lo, head_no * NB_TURN + 2 + NB_TURN)
                weigh(par, 0).then_inc(pv_done, 1)
                project_v(nxt, F_S10 + 3, par, head_no * 6 + 7)

            with pe.Fori(0, B) as b:
                with pe.Fori(0, H // 2) as pair:
                    heads = b * H + pair * 2
                    loads = b * (H // 2) + pair
                    head(heads, 0, loads * 32 + 32)
                    head(heads + 1, 1, loads * 32 + 64)
                pe.wait_ge(y_copied, b + 1)
                zero_y()


def ffn_block(nc, x, y_t, gamma_x, gamma_slot, slots, w1, w2, out):
    B, T, D = x.shape
    N = slots.shape[0] * slots.shape[1]
    F = w1.shape[1]
    NT, NC, FC = T // P, N // P, F // P
    assert D == P and N == BANK and F == BANK and NT == 8 and B % 2 == 0

    with ExitStack() as ctx:
        s = Scope(nc, ctx)
        y_in = s.sb("y_in", [P, T], F32)
        x_row = s.sb("x_row1", [P, NT, D], F32)
        res = s.sb("res", [P, NT, D], F32)
        x1 = [s.sb(f"x1_{i}", [P, NT, D], F32) for i in range(2)]
        z_row = s.sb("z_row", [P, NT, D], F32)
        z = s.sb("z", [P, 2, NT, D], F32R)
        z_t = s.sb("z_t", [P, 2, T], F32R)
        rows_n = s.sb("rows_n", [P, 2, T], F32)
        rows_s = s.sb("rows_s", [P, 4, N], F32)
        disp = s.sb("disp", [P, 2, NT, N], F32R)
        comb = s.sb("comb", [P, 2, NC, T], F32R)
        slot_in = s.sb("slot_in", [P, 2, N], F32R)
        hid = s.sb("hid", [P, FC, N], F32)
        hid_s = s.sb("hid_s", [P, 2, FC, N], F32R)
        proc = s.sb("proc", [P, 2, NC * D], F32R)
        o_t = s.sb("o_t", [P, T], F32)
        res2 = s.sb("res2", [P, NT, D], F32)
        out_row = s.sb("out_row", [P, NT, D], F32)
        stats = s.sb("stats", [P, 2, NT, 6], F32)
        mv = s.sb("mv", [P, 2, NT, 2], F32)
        neg_mean = s.sb("neg_mean", [P, 2, NT], F32)
        rstd = s.sb("rstd", [P, 2, NT], F32)
        power = s.sb("power", [P, 2, NT], F32)
        rms = s.sb("rms", [P, NT], F32)
        minus_half = s.sb("minus_half", [P, NT], F32)
        neg_max = s.sb("neg_max1", [P, 4 + NT], F32)
        sums = s.sb("sums1", [P, 4 + NT], F32)
        inv = s.sb("inv1", [P, 4 + NT], F32)
        ident = s.sb("ident2", [P, P], F32)
        gammas = s.sb("gammas", [P, 2], F32)
        gamma_both = s.sb("gamma_both", [P, 1], F32)
        w1_raw = s.sb("w1_raw", [P, F], F32)
        w2_raw = s.sb("w2_raw", [P, FC, D], F32)
        w1_s = s.sb("w1_s", [P, 2, F], F32R)
        w2_s = s.sb("w2_s", [P, 2, FC, D], F32R)
        se_raw = s.sb("se_raw", [P, NC, D], F32)
        se_sq = s.sb("se_sq", [P, NC, D], F32)
        se_row = s.sb("se_row", [P, NC, D], F32)
        se_t = s.sb("se_t", [P, 2, N], F32R)
        ps_slot = s.ps("ps_slot1", [P, 2, T])
        ps_turn = s.ps("ps_turn1", [P, 2, BANK])
        ps_acc = s.ps("ps_acc", [P, 2, BANK])

        w_landed, in_landed = s.sem("w_landed1"), s.sem("in_landed_f")
        consts, setup, se_norm = s.sem("consts1"), s.sem("setup"), s.sem("se_norm")
        ticks, dve_ticks = s.sem("ticks1"), s.sem("dve_ticks")
        filled, turned = s.sem("filled1"), s.sem("turned1")
        slots_summed, proc_summed = s.sem("slots_summed"), s.sem("proc_summed")
        maxed, inverted = s.sem("maxed1"), s.sem("inverted1")
        added = s.sem("added")
        stats_a, stats_b = s.sem("stats_a"), s.sem("stats_b")
        turn_lo, zt_lo, z_lo = s.sem("turn_lo1"), s.sem("zt_lo"), s.sem("z_lo")
        slot_in_hi, slot_in_lo = s.sem("slot_in_hi"), s.sem("slot_in_lo")
        hid_lo, proc_lo = s.sem("hid_lo"), s.sem("proc_lo")
        exped, turn_hi = s.sem("exped1"), s.sem("turn_hi1")
        zt_hi, z_hi, gelued, hid_hi = s.sem("zt_hi"), s.sem("z_hi"), s.sem("gelued"), s.sem("hid_hi")
        proc_hi, o_copied = s.sem("proc_hi"), s.sem("o_copied")
        normed = s.sem("normed1")
        ln_step, z_made, o_stats = s.sem("ln_step"), s.sem("z_made"), s.sem("o_stats")
        out_made, out_free = s.sem("out_made"), s.sem("out_free")

        ROW_SLOTS = ((0,), (1,), (2,), (3,), (4, 5), (6, 7), (8, 9), (10, 11))
        FILLS = 14
        F_ROWS = (3, 4, 5, 6, 7, 8, 9, 10)
        F_H01, F_H23, F_A1, F_OUT, F_BACK, F_A2 = range(11, 17)

        def slot(fill):
            return ps_slot[:, (fill - 1) % 2, :]

        def row_tile(i, fill):
            if i < 4:
                return slot(fill), rows_n[:, i % 2, :]
            return slot(fill)[:, (i % 2) * BANK:(i % 2 + 1) * BANK], rows_s[:, i % 4, :]

        def turn_view(bank_no, part):
            src = ps_turn[:, bank_no % 2, :].rearrange("p (j c) -> p j c", c=P)
            if bank_no < 8:
                c, half = bank_no // 2, bank_no % 2
                return disp[:, part, 4 * half:4 * half + 4, c * P:(c + 1) * P], src
            t = bank_no - 8
            return comb[:, part, :, t * P:(t + 1) * P], src

        block = ctx.enter_context(nc.Block())

        @block.sync
        def _(sp):
            def load(b):
                sp.dma_start(y_in[:, :], y_t[b, :, :]).then_inc(in_landed, 16)
                sp.dma_start(x_row[:, :, :], x[b, :, :].rearrange("(t p) m -> p t m", p=P)).then_inc(in_landed, 16)

            sp.dma_start(gammas[:, 0:1], gamma_x.rearrange("(p a) -> p a", a=1)).then_inc(w_landed, 16)
            sp.dma_start(gammas[:, 1:2], gamma_slot.rearrange("(p a) -> p a", a=1)).then_inc(w_landed, 16)
            sp.dma_start(se_raw[:, :, :], slots.rearrange("e t d -> (e t) d").rearrange("(c p) d -> p c d", p=P))\
              .then_inc(w_landed, 16)
            load(0)
            sp.dma_start(w1_raw[:, :], w1).then_inc(w_landed, 16)
            sp.dma_start(w2_raw[:, :, :], w2.rearrange("(c p) d -> p c d", p=P)).then_inc(w_landed, 16)

            def batch(b, ahead):
                if ahead:
                    sp.wait_ge(added, b * 2 + 1)
                    load(b + 1)
                sp.wait_ge(out_made, b * NT + NT)
                sp.dma_start(out[b, :, :].rearrange("(t p) m -> p t m", p=P), out_row[:, :, :])\
                  .then_inc(out_free, 16)

            with sp.Fori(0, B - 1) as b:
                batch(b, True)
            batch(B - 1, False)
            sp.wait_ge(out_free, 16 * B + 1)

        @block.gpsimd
        def _(pool):
            pool.memset(ident[:, :], 0.0).then_inc(consts, 1)
            pool.memset(minus_half[:, :], -0.5).then_inc(consts, 1)
            pool.memset(out_row[:, :, :], 0.0).then_inc(out_free, 1)
            pool.wait_ge(consts, 2)
            pool.affine_select(out=ident[:, :], in_=ident[:, :], compare_op=ALU.not_equal, fill=1.0,
                               base=0, pattern=[[-1, P]], channel_multiplier=1).then_inc(consts, 1)

            class Steps:
                at = 0

            def step(ins, base):
                Steps.at += 1
                ins.then_inc(ln_step, 1)
                wait_apart(pool, ln_step, base + Steps.at, ticks)

            def mean_rstd(which, base):
                step(pool.tensor_scalar(neg_mean[:, which, :], mv[:, which, :, 0], -1.0, 1.0, ALU.mult, ALU.mult), base)
                step(pool.tensor_scalar(power[:, which, :], mv[:, which, :, 1], LN_EPS, 1.0, ALU.add, ALU.mult), base)
                step(pool.tensor_tensor(rstd[:, which, :], power[:, which, :], minus_half[:, :], ALU.pow), base)

            def first_norm(par, stats_count, base):
                wait_apart(pool, stats_b, stats_count, ticks)
                mean_rstd(0, base)
                step(pool.tensor_tensor(rms[:, :], mv[:, 0, :, 1], rstd[:, 0, :], ALU.mult), base)
                step(pool.tensor_tensor(rms[:, :], rms[:, :], rstd[:, 0, :], ALU.mult), base)
                step(pool.tensor_scalar(rms[:, :], rms[:, :], float(D), 1e-24, ALU.mult, ALU.max), base)
                step(pool.tensor_tensor(rms[:, :], rms[:, :], minus_half[:, :], ALU.pow), base)
                for t in range(NT):
                    last = pool.tensor_scalar(x1[par][:, t, :], res[:, t, :], neg_mean[:, 0, t:t + 1],
                                              rstd[:, 0, t:t + 1], ALU.add, ALU.mult)
                step(last, base)
                for t in range(NT):
                    pool.tensor_scalar(z_row[:, t, :], x1[par][:, t, :], rms[:, t:t + 1], float(D) ** 0.5,
                                       ALU.mult, ALU.mult).then_inc(z_made, 1)

            def norm_rows(b, i):
                wait_apart(pool, inverted, b * 12 + i + 1, ticks)
                _, row = row_tile(i, 1)
                pool.tensor_scalar(row, row, inv[:, i:i + 1], 1.0, ALU.mult, ALU.mult).then_inc(normed, 1)

            pool.wait_ge(setup, NC)
            step(pool.tensor_scalar(rms[:, 0:NC], rms[:, 0:NC], 1e-24, 1.0, ALU.max, ALU.mult), 0)
            step(pool.tensor_tensor(rms[:, 0:NC], rms[:, 0:NC], minus_half[:, 0:NC], ALU.pow), 0)
            for c in range(NC):
                last = pool.tensor_scalar(se_row[:, c, :], se_raw[:, c, :], rms[:, c:c + 1], float(D) ** 0.5,
                                          ALU.mult, ALU.mult)
            last.then_inc(se_norm, 1)
            pool.wait_ge(se_norm, 1)
            first_norm(0, 1, 0)
            ahead_of_loop = Steps.at
            per_batch = 3 + 8

            def batch(b, par, ahead):
                Steps.at = ahead_of_loop
                base = b * per_batch
                for i in range(12):
                    norm_rows(b, i)
                if ahead:
                    first_norm(1 - par, b + 2, base)
                wait_apart(pool, o_stats, b + 1, ticks)
                mean_rstd(1, base)
                wait_apart(pool, out_free, b * 16 + 1, ticks)
                for t in range(NT):
                    pool.tensor_scalar(out_row[:, t, :], res2[:, t, :], neg_mean[:, 1, t:t + 1],
                                       rstd[:, 1, t:t + 1], ALU.add, ALU.mult).then_inc(out_made, 1)

            with pool.Fori(0, B // 2 - 1) as pair:
                for par in range(2):
                    batch(pair * 2 + par, par, True)
            batch(B - 2, 0, True)
            batch(B - 1, 1, False)

        @block.scalar
        def _(act):
            def exp(b, k):
                for i in ROW_SLOTS[k]:
                    act.wait_ge(maxed, b * 12 + i + 1)
                    src, row = row_tile(i, F_ROWS[k])
                    last = act.activation(row, src, ACT.Exp, bias=neg_max[:, i:i + 1], accum_out=sums[:, i:i + 1])
                last.then_inc(exped, 1)

            def split_turn(b, bank_no):
                act.wait_ge(turned, b * 16 + bank_no + 2)
                dst, src = turn_view(bank_no, 0)
                act.activation(dst, src, ACT.Copy).then_inc(turn_hi, 1)

            def split_z(count):
                act.wait_ge(z_made, count * NT)
                act.activation(z[:, 0, :, :], z_row[:, :, :], ACT.Copy).then_inc(z_hi, 1)

            def split_zt(fill_no, fill):
                act.wait_ge(filled, fill_no)
                act.activation(z_t[:, 0, :], slot(fill), ACT.Copy).then_inc(zt_hi, 1)

            split_z(1)
            split_zt(2, 2)

            def batch(b, ahead):
                exp(b, 0)
                exp(b, 1)
                split_turn(b, 0)
                split_turn(b, 1)
                exp(b, 2)
                split_turn(b, 2)
                split_turn(b, 3)
                exp(b, 3)
                split_turn(b, 4)
                split_turn(b, 5)
                exp(b, 4)
                split_turn(b, 6)
                split_turn(b, 7)
                exp(b, 5)
                split_turn(b, 8)
                split_turn(b, 9)
                exp(b, 6)
                split_turn(b, 10)
                split_turn(b, 11)
                exp(b, 7)
                split_turn(b, 12)
                split_turn(b, 13)
                for c in range(FC):
                    fill = (F_H01, F_H23)[c // 2]
                    if c % 2 == 0:
                        act.wait_ge(filled, b * FILLS + fill)
                    act.activation(hid[:, c, :], slot(fill)[:, (c % 2) * BANK:(c % 2 + 1) * BANK],
                                   ACT.Gelu).then_inc(gelued, 1)
                for c in range(FC):
                    act.wait_ge(gelued, b * FC + c + 1)
                    act.activation(hid_s[:, 0, c, :], hid[:, c, :], ACT.Copy).then_inc(hid_hi, 1)
                split_turn(b, 14)
                split_turn(b, 15)
                act.wait_ge(proc_summed, b + 1)
                act.activation(proc[:, 0, :], ps_acc[:, 1, :], ACT.Copy).then_inc(proc_hi, 1)
                act.wait_ge(filled, b * FILLS + F_OUT - (0 if ahead else 1))
                act.activation(o_t[:, :], slot(F_OUT), ACT.Copy).then_inc(o_copied, 1)
                if ahead:
                    split_z(b + 2)
                    split_zt(b * FILLS + F_A2, F_A2)

            with act.Fori(0, B - 1) as b:
                batch(b, True)
            batch(B - 1, False)

        @block.vector
        def _(dve):
            dve.wait_ge(w_landed, 80)
            for c in range(NC):
                dve.tensor_tensor_reduce(se_sq[:, c, :], se_raw[:, c, :], se_raw[:, c, :], 1.0, 0.0,
                                         ALU.mult, ALU.add, rms[:, c:c + 1]).then_inc(setup, 1)
            dve.tensor_tensor(gamma_both[:, :], gammas[:, 0:1], gammas[:, 1:2], ALU.mult).then_inc(setup, 1)
            dve.tensor_copy(w1_s[:, 0, :], w1_raw[:, :]).then_inc(setup, 1)
            dve.tensor_copy(w2_s[:, 0, :, :], w2_raw[:, :, :]).then_inc(setup, 1)
            dve.wait_ge(setup, NC + 3)
            dve.tensor_tensor(w1_s[:, 1, :], w1_raw[:, :], f32(w1_s[:, 0, :]), ALU.subtract).then_inc(setup, 1)
            dve.tensor_tensor(w2_s[:, 1, :, :], w2_raw[:, :, :], f32(w2_s[:, 0, :, :]), ALU.subtract)\
               .then_inc(setup, 1)
            dve.wait_ge(turned, 1)
            dve.tensor_scalar(se_t[:, 0, :], ps_turn[:, 0, :], gamma_both[:, 0:1], None, ALU.mult).then_inc(setup, 1)
            dve.wait_ge(setup, NC + 6)
            dve.scalar_tensor_tensor(se_t[:, 1, :], ps_turn[:, 0, :], gamma_both[:, 0:1], f32(se_t[:, 0, :]),
                                     ALU.mult, ALU.subtract).then_inc(turn_lo, 1)
            dve.memset(neg_max[:, :], 0.0).then_inc(turn_lo, 1)
            dve.wait_ge(turn_lo, 2)

            def add_stats(fill_no, fill, other, dst, which, stats_count, done):
                dve.wait_ge(filled, fill_no)
                dve.tensor_tensor(dst[:, :, :], slot(fill).rearrange("p (t m) -> p t m", m=D), other[:, :, :],
                                  ALU.add).then_inc(added, 1)
                dve.wait_ge(added, stats_count)
                for t in range(NT):
                    last = dve.bn_stats(stats[:, which, t, :], dst[:, t, :])
                last.then_inc(stats_a, 1)
                wait_apart(dve, stats_a, stats_count, dve_ticks)
                for t in range(NT):
                    last = dve.bn_aggr(mv[:, which, t, :], stats[:, which, t, :])
                last.then_inc(done, 1)

            def split_zt(count, fill):
                dve.wait_ge(zt_hi, count)
                dve.tensor_tensor(z_t[:, 1, :], slot(fill), f32(z_t[:, 0, :]), ALU.subtract).then_inc(zt_lo, 1)

            def split_z(count):
                dve.wait_ge(z_hi, count)
                dve.tensor_tensor(z[:, 1, :, :], z_row[:, :, :], f32(z[:, 0, :, :]), ALU.subtract).then_inc(z_lo, 1)

            def rowmax(b, k):
                dve.wait_ge(filled, b * FILLS + F_ROWS[k])
                for i in ROW_SLOTS[k]:
                    src, _ = row_tile(i, F_ROWS[k])
                    dve.tensor_reduce(neg_max[:, i:i + 1], src, AX.X, ALU.max, negate=True).then_inc(maxed, 1)

            def invert(b, k):
                dve.wait_ge(exped, b * 8 + k + 1)
                for i in ROW_SLOTS[k]:
                    dve.reciprocal(inv[:, i:i + 1], sums[:, i:i + 1]).then_inc(inverted, 1)

            def split_turn(b, bank_no):
                dve.wait_ge(turn_hi, b * 16 + bank_no + 1)
                dst, src = turn_view(bank_no, 1)
                dve.tensor_tensor(dst, src, f32(turn_view(bank_no, 0)[0]), ALU.subtract).then_inc(turn_lo, 1)

            dve.wait_ge(in_landed, 32)
            add_stats(1, 1, x_row, res, 0, 1, stats_b)
            split_z(1)
            split_zt(1, 2)

            def batch(b, par, ahead):
                rowmax(b, 0)
                rowmax(b, 1)
                invert(b, 0)
                invert(b, 1)
                for k in range(2, 8):
                    rowmax(b, k)
                    split_turn(b, 2 * k - 4)
                    split_turn(b, 2 * k - 3)
                    invert(b, k)
                    if k == 6:
                        dve.wait_ge(slots_summed, b + 1)
                        dve.tensor_scalar(slot_in[:, 0, :], ps_acc[:, 0, :], gammas[:, 0:1], None,
                                          ALU.mult).then_inc(slot_in_hi, 1)
                        dve.wait_ge(slot_in_hi, b + 1)
                        dve.scalar_tensor_tensor(slot_in[:, 1, :], ps_acc[:, 0, :], gammas[:, 0:1],
                                                 f32(slot_in[:, 0, :]), ALU.mult, ALU.subtract).then_inc(slot_in_lo, 1)
                split_turn(b, 12)
                split_turn(b, 13)
                for c in range(FC):
                    dve.wait_ge(hid_hi, b * FC + c + 1)
                    dve.tensor_tensor(hid_s[:, 1, c, :], hid[:, c, :], f32(hid_s[:, 0, c, :]),
                                      ALU.subtract).then_inc(hid_lo, 1)
                split_turn(b, 14)
                split_turn(b, 15)
                if ahead:
                    dve.wait_ge(in_landed, b * 32 + 64)
                    add_stats(b * FILLS + F_A1, F_A1, x_row, res, 0, b * 2 + 2, stats_b)
                dve.wait_ge(proc_hi, b + 1)
                dve.tensor_tensor(proc[:, 1, :], ps_acc[:, 1, :], f32(proc[:, 0, :]), ALU.subtract).then_inc(proc_lo, 1)
                add_stats(b * FILLS + F_BACK - (0 if ahead else 1), F_BACK, x1[par], res2, 1,
                          b * 2 + (3 if ahead else 2), o_stats)
                if ahead:
                    split_z(b + 2)
                    split_zt(b + 2, F_A2)

            with dve.Fori(0, B // 2 - 1) as pair:
                for par in range(2):
                    batch(pair * 2 + par, par, True)
            batch(B - 2, 0, True)
            batch(B - 1, 1, False)

        @block.tensor
        def _(pe):
            pe.wait_ge(consts, 3)

            def transposes(src, fill):
                for t in range(NT):
                    last = pe.transpose(slot(fill)[:, t * P:(t + 1) * P], src(t), ident[:, :])
                last.then_inc(filled, 1)

            def rows(k):
                for i in ROW_SLOTS[k]:
                    dst, _ = row_tile(i, F_ROWS[k])
                    if i < 4:
                        own = slice(i * P, (i + 1) * P)
                        for c in range(2):
                            cols = slice(c * BANK, (c + 1) * BANK)
                            last = matmul_split(pe, dst[:, cols], se_t[:, 0, own], se_t[:, 1, own],
                                                z_t[:, 0, cols], z_t[:, 1, cols], True, True)
                    else:
                        own = slice((i - 4) * P, (i - 3) * P)
                        last = matmul_split(pe, dst, z_t[:, 0, own], z_t[:, 1, own],
                                            se_t[:, 0, :], se_t[:, 1, :], True, True)
                last.then_inc(filled, 1)

            def turn(b, k):
                for n, i in enumerate(ROW_SLOTS[k]):
                    pe.wait_ge(normed, b * 12 + i + 1)
                    _, row = row_tile(i, 1)
                    for half in range(len(ROW_SLOTS[k]) % 2 + 1):
                        bank_no = 2 * k + n + half
                        pe.wait_ge(turn_lo, b * 16 + bank_no + 1)
                        for j in range(4):
                            last = pe.transpose(ps_turn[:, bank_no % 2, j * P:(j + 1) * P],
                                                row[:, (4 * half + j) * P:(4 * half + j + 1) * P], ident[:, :])
                        last.then_inc(turned, 1)

            pe.wait_ge(in_landed, 32)
            transposes(lambda t: y_in[:, t * P:(t + 1) * P], 1)
            pe.wait_ge(se_norm, 1)
            for c in range(NC):
                last = pe.transpose(ps_turn[:, 0, c * P:(c + 1) * P], se_row[:, c, :], ident[:, :])
            last.then_inc(turned, 1)
            pe.wait_ge(z_made, NT)
            transposes(lambda t: z_row[:, t, :], 2)

            def batch(b, ahead):
                pe.wait_ge(zt_lo, b + 1)
                pe.wait_ge(added, b * 2 + 1)
                rows(0)
                rows(1)
                turn(b, 0)
                for k in range(2, 6):
                    pe.wait_ge(exped, b * 8 + k - 1)
                    rows(k)
                    turn(b, k - 1)
                pe.wait_ge(turn_lo, b * 16 + 8 + 2)
                pe.wait_ge(z_lo, b + 1)
                for t in range(NT):
                    last = matmul_split(pe, ps_acc[:, 0, :], z[:, 0, t, :], z[:, 1, t, :],
                                        disp[:, 0, t, :], disp[:, 1, t, :], t == 0, t == NT - 1)
                last.then_inc(slots_summed, 1)
                for k in range(6, 8):
                    pe.wait_ge(exped, b * 8 + k - 1)
                    rows(k)
                    turn(b, k - 1)
                for c in range(FC):
                    fill = (F_H01, F_H23)[c // 2]
                    if c % 2 == 0:
                        pe.wait_ge(exped, b * 8 + 7 + c // 2)
                    if c == 0:
                        pe.wait_ge(slot_in_lo, b + 1)
                    own = slice(c * P, (c + 1) * P)
                    last = matmul_split(pe, slot(fill)[:, (c % 2) * BANK:(c % 2 + 1) * BANK],
                                        w1_s[:, 0, own], w1_s[:, 1, own], slot_in[:, 0, :], slot_in[:, 1, :],
                                        True, True)
                    if c % 2 == 1:
                        last.then_inc(filled, 1)
                turn(b, 7)
                if ahead:
                    pe.wait_ge(in_landed, b * 32 + 64)
                    pe.wait_ge(gelued, b * FC + 2)
                    transposes(lambda t: y_in[:, t * P:(t + 1) * P], F_A1)
                pe.wait_ge(hid_lo, b * FC + FC)
                for n in range(NC):
                    own = slice(n * P, (n + 1) * P)
                    for c in range(FC):
                        last = matmul_split(pe, ps_acc[:, 1, own], hid_s[:, 0, c, own], hid_s[:, 1, c, own],
                                            w2_s[:, 0, c, :], w2_s[:, 1, c, :], c == 0, c == FC - 1)
                last.then_inc(proc_summed, 1)
                pe.wait_ge(proc_lo, b + 1)
                pe.wait_ge(turn_lo, b * 16 + 16 + 2)
                pe.wait_ge(gelued, b * FC + FC)
                for h in range(2):
                    cols = slice(h * BANK, (h + 1) * BANK)
                    for c in range(NC):
                        own = slice(c * P, (c + 1) * P)
                        last = matmul_split(pe, slot(F_OUT)[:, cols], proc[:, 0, own], proc[:, 1, own],
                                            comb[:, 0, c, cols], comb[:, 1, c, cols], c == 0, c == NC - 1)
                last.then_inc(filled, 1)
                pe.wait_ge(o_copied, b + 1)
                if ahead:
                    pe.wait_ge(added, b * 2 + 2)
                transposes(lambda t: o_t[:, t * P:(t + 1) * P], F_BACK)
                if ahead:
                    pe.wait_ge(z_made, b * NT + 2 * NT)
                    transposes(lambda t: z_row[:, t, :], F_A2)

            with pe.Fori(0, B - 1) as b:
                batch(b, True)
            batch(B - 1, False)


def build(nc, x, wq, wk, wv, wo, gamma_x, gamma_slot, slots, w1, w2, rope_c, rope_s, out):
    B, T, M = x.shape
    H = wq.shape[1]
    w_split = nc.dram_tensor("w_split", (H, M, 6, P), F32, kind="Internal").ap()
    x_split = nc.dram_tensor("x_split", (B + 1, M, 2, T), F32, kind="Internal").ap()
    y_t = nc.dram_tensor("y_t", (B, M, T), F32, kind="Internal").ap()
    prepare_block(nc, x, wq, wk, wv, wo, w_split, x_split)
    attention_block(nc, w_split, x_split, rope_c, rope_s, y_t, B, H, T)
    ffn_block(nc, x, y_t, gamma_x, gamma_slot, slots, w1, w2, out)


_INS = ["L0_attn_x", "L0_attn_wq", "L0_attn_wk", "L0_attn_wv", "L0_attn_wo", "L0_ffn_gamma_x",
        "L0_ffn_gamma_slot", "L0_ffn_slot_embeds", "L0_ffn_w1", "L0_ffn_w2"]


def kernel(**inputs):
    import concourse.bacc as _bacc
    from concourse.bass_utils import run_bass_kernel_spmd as _run

    nc = _bacc.Bacc("TRN2", target_bir_lowering=False, num_devices=1)
    arrays = {f"in_{name}": np.ascontiguousarray(inputs[name]) for name in _INS}
    shape = arrays["in_L0_attn_x"].shape
    arrays["rope_c"], arrays["rope_s"] = rope_tables(shape[1], inputs["L0_attn_wq"].shape[2])
    args = [nc.dram_tensor(n, a.shape, mybir.dt.from_np(a.dtype), kind="ExternalInput").ap()
            for n, a in arrays.items()]
    out = nc.dram_tensor("out_0", shape, F32, kind="ExternalOutput").ap()
    build(nc, *args, out)
    r = _run(nc, [arrays], core_ids=[0])
    return r.results[0]["out_0"]
```

```python
from contextlib import ExitStack

import numpy as np

import concourse.bass as bass
from concourse import mybir

P = 128
BANK = 512
ALU = mybir.AluOpType
ACT = mybir.ActivationFunctionType
AX = mybir.AxisListType
F32 = mybir.dt.float32
F32R = mybir.dt.float32r
BF16 = mybir.dt.bfloat16
ROTARY_BASE = 10000.0
MASKED = -1e30
LN_EPS = 1e-5

WQ_HI, WQ_LO, WK_HI, WK_LO, WVO = range(5)
NW = 5
X_HI, X_LO, X_WHOLE = range(3)
NX = 3


class Scope:

    def __init__(self, nc, ctx):
        self.nc, self.ctx = nc, ctx

    def sb(self, name, shape, dt):
        return self.ctx.enter_context(self.nc.sbuf_tensor(name, shape, dt))

    def ps(self, name, shape):
        return self.ctx.enter_context(self.nc.psum_tensor(name, shape, F32))

    def sem(self, name):
        return self.ctx.enter_context(self.nc.semaphore(name))


def matmul_split(pe, out, stat_hi, stat_lo, mov_hi, mov_lo, start, stop):
    pe.matmul(out, stat_hi, mov_hi, start=start, stop=False, skip_group_check=True)
    pe.matmul(out, stat_hi, mov_lo, start=False, stop=False, skip_group_check=True)
    return pe.matmul(out, stat_lo, mov_hi, start=False, stop=stop, skip_group_check=True)


def wait_apart(eng, sem, value, ticks):
    eng.wait_ge(sem, value)
    eng.sem_inc(ticks, 1)


def f32(ap):
    return ap.bitcast(F32)


def prepare_block(nc, x, wq, wk, wv, wo, w_split, x_split):
    B, T, M = x.shape
    H = wq.shape[1]
    NT = T // P
    with ExitStack() as ctx:
        s = Scope(nc, ctx)
        w_raw = s.sb("w_raw", [P, 4, H * P], F32)
        wv_t = s.sb("wv_t", [P, H, P], F32)
        w_out = s.sb("w_out", [P, H, 4, P], F32R)
        wvo = s.sb("wvo", [P, H, P], F32)
        x_row = s.sb("x_row", [P, 2, NT, M], F32)
        x_out = s.sb("x_out", [P, 2, 2, T], F32R)
        x_whole = s.sb("x_whole", [P, 2, T], F32)
        ident = s.sb("ident0", [P, P], F32)
        ps_w = s.ps("ps_w", [P, 2, H * P])
        ps_x = s.ps("ps_x", [P, 2, T])
        ident_made = s.sem("ident_made0")
        w_landed = s.sem("w_landed")
        qk_split = s.sem("qk_split")
        wv_turned, wv_copied = s.sem("wv_turned"), s.sem("wv_copied")
        wvo_made, wvo_copied = s.sem("wvo_made"), s.sem("wvo_copied")
        x_landed = [s.sem(f"x_landed{i}") for i in range(2)]
        x_turned, x_hi, x_lo, x_copied = s.sem("x_turned"), s.sem("x_hi"), s.sem("x_lo"), s.sem("x_copied")
        x_stored = [s.sem(f"x_stored{i}") for i in range(2)]
        w_stored = s.sem("w_stored")

        block = ctx.enter_context(nc.Block())

        @block.sync
        def _(sp):
            for i, w in enumerate((wq, wk, wv)):
                sp.dma_start(w_raw[:, i, :], w.rearrange("m h d -> m (h d)")).then_inc(w_landed, 16)
            sp.dma_start(w_raw[:, 3, :].rearrange("p (h m) -> p h m", h=H),
                         wo.rearrange("h d m -> d h m")).then_inc(w_landed, 16)
            sp.wait_ge(qk_split, 4)
            out = w_split.rearrange("h m s d -> m h s d")
            sp.dma_start(out[:, :, 0:WVO, :], f32(w_out[:, :, :, :])).then_inc(w_stored, 16)
            sp.wait_ge(wvo_copied, 1)
            sp.dma_start(out[:, :, WVO, :], wvo[:, :, :]).then_inc(w_stored, 16)
            sp.wait_ge(w_stored, 32)

        @block.gpsimd
        def _(pool):
            pool.memset(ident[:, :], 0.0).then_inc(ident_made, 1)
            pool.wait_ge(ident_made, 1)
            pool.affine_select(out=ident[:, :], in_=ident[:, :], compare_op=ALU.not_equal, fill=1.0,
                               base=0, pattern=[[-1, P]], channel_multiplier=1).then_inc(ident_made, 1)

        @block.scalar
        def _(act):
            def load(b):
                act.dma_start(x_row[:, b % 2, :, :],
                              x[b, :, :].rearrange("(t p) m -> p t m", p=P)).then_inc(x_landed[b % 2], 16)

            load(0)
            load(1)
            act.wait_ge(wv_turned, 1)
            act.activation(wv_t[:, :, :], ps_w[:, 0, :].rearrange("p (h m) -> p h m", h=H),
                           ACT.Copy).then_inc(wv_copied, 1)
            for b in range(B):
                act.wait_ge(x_turned, b + 1)
                if b + 2 < B:
                    load(b + 2)
                if b >= 2:
                    act.wait_ge(x_stored[b % 2], 32 * (b // 2))
                act.activation(x_whole[:, b % 2, :], ps_x[:, b % 2, :], ACT.Copy).then_inc(x_copied, 1)
                act.wait_ge(x_copied, b + 1)
                act.activation(x_out[:, b % 2, 0, :], x_whole[:, b % 2, :], ACT.Copy).then_inc(x_hi, 1)
                act.wait_ge(x_lo, b + 1)
                for at in (b, B) if b == B - 1 else (b,):
                    act.dma_start(x_split[at, :, 0:X_WHOLE, :], f32(x_out[:, b % 2, :, :])).then_inc(x_stored[b % 2], 16)
                    act.dma_start(x_split[at, :, X_WHOLE, :], x_whole[:, b % 2, :]).then_inc(x_stored[b % 2], 16)
            act.wait_ge(x_stored[0], 32 * (B // 2))
            act.wait_ge(x_stored[1], 32 * (B // 2 + 1))

        @block.vector
        def _(dve):
            dve.wait_ge(w_landed, 64)
            for i, (hi, lo, scale) in enumerate(((WQ_HI, WQ_LO, 1.0 / P), (WK_HI, WK_LO, 1.0))):
                raw = w_raw[:, i, :].rearrange("p (h d) -> p h d", h=H)
                dve.tensor_scalar(w_out[:, :, hi, :], raw, scale, None, ALU.mult).then_inc(qk_split, 1)
                dve.wait_ge(qk_split, 2 * i + 1)
                dve.scalar_tensor_tensor(w_out[:, :, lo, :], raw, scale, f32(w_out[:, :, hi, :]),
                                         ALU.mult, ALU.subtract).then_inc(qk_split, 1)
            dve.wait_ge(wvo_made, 1)
            dve.tensor_copy(wvo[:, :, :], ps_w[:, 1, :].rearrange("p (h m) -> p h m", h=H)).then_inc(wvo_copied, 1)
            for b in range(B):
                dve.wait_ge(x_hi, b + 1)
                dve.tensor_tensor(x_out[:, b % 2, 1, :], x_whole[:, b % 2, :], f32(x_out[:, b % 2, 0, :]),
                                  ALU.subtract).then_inc(x_lo, 1)

        @block.tensor
        def _(pe):
            pe.wait_ge(ident_made, 2)
            pe.wait_ge(w_landed, 64)
            for h in range(H):
                last = pe.transpose(ps_w[:, 0, h * P:(h + 1) * P], w_raw[:, 2, h * P:(h + 1) * P], ident[:, :])
            last.then_inc(wv_turned, 1)
            pe.wait_ge(wv_copied, 1)
            for h in range(H):
                last = pe.matmul(ps_w[:, 1, h * P:(h + 1) * P], wv_t[:, h, :],
                                 w_raw[:, 3, h * P:(h + 1) * P], start=True, stop=True)
            last.then_inc(wvo_made, 1)
            for b in range(B):
                pe.wait_ge(x_landed[b % 2], 16 * (b // 2 + 1))
                if b >= 2:
                    pe.wait_ge(x_copied, b - 1)
                for t in range(NT):
                    last = pe.transpose(ps_x[:, b % 2, t * P:(t + 1) * P], x_row[:, b % 2, t, :], ident[:, :])
                last.then_inc(x_turned, 1)


def rope_tables(T, D):
    half = D // 2
    freq = np.power(np.float32(ROTARY_BASE), -np.arange(half, dtype=np.float32) / np.float32(half))
    ang = (np.arange(T, dtype=np.float32)[:, None] * freq.astype(np.float32)[None, :]).T
    cos, sin = np.cos(ang).astype(np.float32), np.sin(ang).astype(np.float32)
    return np.concatenate([cos, cos]), np.concatenate([-sin, sin])


SLOT_TILES = ((7,), (6,), (5,), (4,), (3, 2), (1, 0))
TILES = (7, 6, 5, 4, 3, 2, 1, 0)
TURN_BANKS = tuple(
    [(s, [(t, 0, 4)]) if half == 0 else (s, [(t, 4, t + 1)])
     for s, t in enumerate((7, 6, 5, 4)) for half in range(2)]
    + [(4, [(3, 0, 4)]), (4, [(2, 0, 3)]), (5, [(1, 0, 2), (0, 0, 1)])])
NB_TURN = len(TURN_BANKS)
BANKS_HIGH = 8
FILLS = 9
F_V0 = 3
F_S7, F_S6, F_Q, F_S5, F_K, F_S4, F_S32, F_V, F_S10, F_S7_NEXT, F_S6_NEXT = range(4, 15)
SCORE_FILLS = (F_S7, F_S6, F_S5, F_S4, F_S32, F_S10)


def attention_block(nc, w_split, x_split, rope_c, rope_s, y_t, B, H, T):
    NT = T // P
    D = P
    assert NT == 8 and H % 2 == 0
    width = {t: P * (t + 1) for t in TILES}
    p_at, at = {}, 0
    for t in TILES:
        p_at[t] = at
        at += width[t]
    stat_col = {t: i for i, t in enumerate(TILES)}

    with ExitStack() as ctx:
        s = Scope(nc, ctx)
        rope = s.sb("rope", [P, 2, T], F32)
        w_in = [s.sb(f"w_in{i}", [P, 4, D], F32R) for i in range(2)]
        wvo_in = [s.sb(f"wvo_in{i}", [P, D], F32) for i in range(2)]
        x_in = [s.sb(f"x_in{i}", [P, 2, T], F32R) for i in range(2)]
        xw_in = [s.sb(f"xw_in{i}", [P, T], F32) for i in range(2)]
        qk = [[s.sb(f"{n}{i}", [P, 2, T], F32R) for n in "qk"] for i in range(2)]
        v_in = [s.sb(f"v{i}", [P, T], F32) for i in range(2)]
        unrot = [s.sb(f"unrot_{n}", [P, T], F32) for n in "qk"]
        swapped = [s.sb(f"swapped_{n}", [P, T], F32) for n in "qk"]
        probs = s.sb("probs", [P, at], F32)
        pt = [s.sb("pt_low", [P, 4, BANK], F32), s.sb("pt_high", [P, 8, BANK], F32)]
        y_out = s.sb("y_out", [P, T], F32)
        neg_max = s.sb("neg_max", [P, 2, NT], F32)
        sums = s.sb("sums", [P, 2, NT], F32)
        inv = s.sb("inv", [P, 2, NT], F32)
        ident = s.sb("ident1", [P, P], F32)
        ident_b = s.sb("ident_b", [P, P], BF16)
        mask_b = s.sb("mask_b", [P, P], BF16)
        zeros_b = s.sb("zeros_b", [P, BANK], BF16)
        ps_slot = s.ps("ps_slot", [P, 2, T])
        ps_turn = s.ps("ps_turn", [P, 2, BANK])
        ps_y = s.ps("ps_y", [P, 2, BANK])

        consts, ticks = s.sem("consts"), s.sem("ticks")
        rope_landed = s.sem("rope_landed")
        w_landed = [s.sem(f"w_landed{i}") for i in range(2)]
        x_landed = [s.sem(f"x_landed_a{i}") for i in range(2)]
        filled = s.sem("filled")
        turned = s.sem("turned")
        pv_done = s.sem("pv_done")
        maxed = s.sem("maxed")
        inverted = s.sem("inverted")
        v_copied, rot_mul, qk_lo = s.sem("v_copied"), s.sem("rot_mul"), s.sem("qk_lo")
        exped = s.sem("exped")
        qk_raw, qk_hi, turn_copied = s.sem("qk_raw"), s.sem("qk_hi"), s.sem("turn_copied")
        y_copied, y_free = s.sem("y_copied"), s.sem("y_free")
        normed = s.sem("normed")
        rot_sum = s.sem("rot_sum")
        swap_landed = [s.sem(f"swap_landed_{n}") for n in "qk"]

        def slot(fill, par):
            return ps_slot[:, (fill + par * FILLS - 1) % 2, :]

        def turn_views(bank_no, par):
            at = 0
            bank = (bank_no + par * NB_TURN) % 2
            for t, j0, j1 in TURN_BANKS[bank_no][1]:
                c = (t % 4) * P
                src = ps_turn[:, bank, at:at + (j1 - j0) * P].rearrange("p (j c) -> p j c", c=P)
                yield pt[t // 4][:, j0:j1, c:c + P], src
                at += (j1 - j0) * P

        block = ctx.enter_context(nc.Block())

        @block.sync
        def _(sp):
            def load_w(head, par):
                sp.dma_start(f32(w_in[par][:, :, :]), w_split[head, :, 0:WVO, :]).then_inc(w_landed[par], 16)
                sp.dma_start(wvo_in[par][:, :], w_split[head, :, WVO, :]).then_inc(w_landed[par], 16)

            def load_x(batch, par):
                sp.dma_start(f32(x_in[par][:, :, :]), x_split[batch, :, 0:X_WHOLE, :]).then_inc(x_landed[par], 16)
                sp.dma_start(xw_in[par][:, :], x_split[batch, :, X_WHOLE, :]).then_inc(x_landed[par], 16)

            def swap(which, raw_count):
                sp.wait_ge(qk_raw, raw_count)
                for half in range(2):
                    sp.dma_start(swapped[which][64 * half:64 * half + 64, :],
                                 unrot[which][64 - 64 * half:128 - 64 * half, :]).then_inc(swap_landed[which], 16)

            load_w(0, 0)
            load_x(0, 0)
            sp.dma_start(rope[:, 0, :], rope_c).then_inc(rope_landed, 16)
            sp.dma_start(rope[:, 1, :], rope_s).then_inc(rope_landed, 16)
            load_w(1, 1)
            load_x(0, 1)
            swap(0, 1)
            swap(1, 2)

            def head(head_no, par, next_w, next_x):
                sp.wait_ge(filled, head_no * FILLS + F_S6)
                load_w(next_w, par)
                if next_x is None:
                    sp.sem_inc(x_landed[par], 32)
                else:
                    load_x(next_x, par)
                swap(0, head_no * 2 + 3)
                swap(1, head_no * 2 + 4)

            with sp.Fori(0, B) as b:
                with sp.Fori(0, H // 2 - 1) as pair:
                    for par in range(2):
                        head(b * H + pair * 2 + par, par, pair * 2 + 2 + par, None)
                for par in range(2):
                    head(b * H + (H - 2 + par), par, par, b + 1)
                sp.wait_ge(y_copied, b + 1)
                sp.dma_start(y_t[b, :, :], y_out[:, :]).then_inc(y_free, 16)
            sp.wait_ge(y_free, 16 * B + 1)
            for par in range(2):
                sp.wait_ge(w_landed[par], 32 * (B * H // 2 + 1))
                sp.wait_ge(x_landed[par], 32 * (B * H // 2 + 1))

        @block.gpsimd
        def _(pool):
            pool.memset(ident[:, :], 0.0).then_inc(consts, 1)
            pool.memset(ident_b[:, :], 0.0).then_inc(consts, 1)
            pool.memset(mask_b[:, :], 0.0).then_inc(consts, 1)
            pool.memset(zeros_b[:, :], 0.0).then_inc(consts, 1)
            pool.memset(y_out[:, :], 0.0).then_inc(y_free, 1)
            pool.wait_ge(consts, 4)
            for m in (ident, ident_b):
                pool.affine_select(out=m[:, :], in_=m[:, :], compare_op=ALU.not_equal, fill=1.0,
                                   base=0, pattern=[[-1, P]], channel_multiplier=1).then_inc(consts, 1)
            pool.affine_select(out=mask_b[:, :], in_=mask_b[:, :], compare_op=ALU.is_ge, fill=MASKED,
                               base=0, pattern=[[-1, P]], channel_multiplier=1).then_inc(consts, 1)

            def rotate(which, count):
                pool.wait_ge(rot_mul, count * 2)
                pool.tensor_tensor(unrot[which][:, :], unrot[which][:, :], swapped[which][:, :],
                                   ALU.add).then_inc(rot_sum, 1)

            def norm(head_no, par, slot_no):
                wait_apart(pool, inverted, head_no * 6 + slot_no + 1, ticks)
                for t in SLOT_TILES[slot_no]:
                    tile = probs[:, p_at[t]:p_at[t] + width[t]]
                    pool.tensor_scalar(tile, tile, inv[:, par, stat_col[t]:stat_col[t] + 1], 1.0,
                                       ALU.mult, ALU.mult).then_inc(normed, 1)

            rotate(0, 1)
            rotate(1, 2)

            def head(head_no, par):
                norm(head_no, par, 0)
                norm(head_no, par, 1)
                norm(head_no, par, 2)
                norm(head_no, par, 3)
                rotate(0, head_no * 2 + 3)
                norm(head_no, par, 4)
                norm(head_no, par, 5)
                rotate(1, head_no * 2 + 4)

            with pool.Fori(0, B) as b:
                with pool.Fori(0, H // 2) as pair:
                    for par in range(2):
                        head(b * H + pair * 2 + par, par)

        @block.scalar
        def _(act):
            def exp(head_no, par, slot_no):
                for i, t in enumerate(SLOT_TILES[slot_no]):
                    c = stat_col[t]
                    act.wait_ge(maxed, head_no * NT + c + 1)
                    src = slot(SCORE_FILLS[slot_no], par)[:, i * BANK:i * BANK + width[t]]
                    last = act.activation(probs[:, p_at[t]:p_at[t] + width[t]], src, ACT.Exp,
                                          bias=neg_max[:, par, c:c + 1], accum_out=sums[:, par, c:c + 1])
                last.then_inc(exped, 1)

            def raw(which, fill_no, fill, par):
                act.wait_ge(filled, fill_no)
                act.activation(unrot[which][:, :], slot(fill, par), ACT.Copy).then_inc(qk_raw, 1)

            def split_hi(which, par, count):
                act.wait_ge(rot_sum, count)
                act.activation(qk[par][which][:, 0, :], unrot[which][:, :], ACT.Copy).then_inc(qk_hi, 1)

            def copy_turn(head_no, par, bank_no):
                act.wait_ge(turned, head_no * NB_TURN + bank_no + 1)
                for dst, src in turn_views(bank_no, par):
                    last = act.activation(dst, src, ACT.Copy)
                last.then_inc(turn_copied, 1)

            act.sem_inc(turn_copied, 2)
            raw(0, 1, 1, 0)
            raw(1, 2, 2, 0)
            split_hi(0, 0, 1)
            split_hi(1, 0, 2)

            def head(head_no, par):
                nxt = 1 - par
                exp(head_no, par, 0)
                exp(head_no, par, 1)
                act.wait_ge(qk_lo, head_no * 2 + 1)
                raw(0, head_no * FILLS + F_Q, F_Q, par)
                copy_turn(head_no, par, 0)
                copy_turn(head_no, par, 1)
                exp(head_no, par, 2)
                copy_turn(head_no, par, 2)
                copy_turn(head_no, par, 3)
                act.wait_ge(qk_lo, head_no * 2 + 2)
                raw(1, head_no * FILLS + F_K, F_K, par)
                exp(head_no, par, 3)
                copy_turn(head_no, par, 4)
                copy_turn(head_no, par, 5)
                exp(head_no, par, 4)
                copy_turn(head_no, par, 6)
                copy_turn(head_no, par, 7)
                exp(head_no, par, 5)
                split_hi(0, nxt, head_no * 2 + 3)
                copy_turn(head_no, par, 8)
                copy_turn(head_no, par, 9)
                copy_turn(head_no, par, 10)
                split_hi(1, nxt, head_no * 2 + 4)

            with act.Fori(0, B) as b:
                with act.Fori(0, H // 2) as pair:
                    for par in range(2):
                        head(b * H + pair * 2 + par, par)
                act.wait_ge(pv_done, b * H + H)
                act.wait_ge(y_free, b * 16 + 1)
                act.activation(y_out[:, :].rearrange("p (g c) -> p g c", g=2), ps_y[:, :, :],
                               ACT.Copy).then_inc(y_copied, 1)

        @block.vector
        def _(dve):
            dve.wait_ge(rope_landed, 32)

            def rowmax(head_no, par, slot_no):
                fill = SCORE_FILLS[slot_no]
                dve.wait_ge(filled, head_no * FILLS + fill)
                for i, t in enumerate(SLOT_TILES[slot_no]):
                    c = stat_col[t]
                    dve.tensor_reduce(neg_max[:, par, c:c + 1], slot(fill, par)[:, i * BANK:i * BANK + width[t]],
                                      AX.X, ALU.max, negate=True).then_inc(maxed, 1)

            def invert(head_no, par, slot_no):
                dve.wait_ge(exped, head_no * 6 + slot_no + 1)
                c = stat_col[SLOT_TILES[slot_no][0]]
                n = len(SLOT_TILES[slot_no])
                dve.reciprocal(inv[:, par, c:c + n], sums[:, par, c:c + n]).then_inc(inverted, 1)

            def rotate_mul_cos(which, count):
                dve.wait_ge(swap_landed[which], count * 32)
                dve.tensor_tensor(unrot[which][:, :], unrot[which][:, :], rope[:, 0, :], ALU.mult).then_inc(rot_mul, 1)

            def rotate_mul_sin(which):
                dve.tensor_tensor(swapped[which][:, :], swapped[which][:, :], rope[:, 1, :],
                                  ALU.mult).then_inc(rot_mul, 1)

            def split_lo(which, par, count):
                dve.wait_ge(qk_hi, count)
                dve.tensor_tensor(qk[par][which][:, 1, :], unrot[which][:, :], f32(qk[par][which][:, 0, :]),
                                  ALU.subtract).then_inc(qk_lo, 1)

            def copy_v(fill_no, fill, par, v_par):
                dve.wait_ge(filled, fill_no)
                dve.tensor_copy(v_in[v_par][:, :], slot(fill, par)).then_inc(v_copied, 1)

            rotate_mul_cos(0, 1)
            rotate_mul_sin(0)
            copy_v(F_V0, F_V0, 0, 0)
            rotate_mul_cos(1, 1)
            rotate_mul_sin(1)
            split_lo(0, 0, 1)
            split_lo(1, 0, 2)

            def head(head_no, par):
                nxt = 1 - par
                rowmax(head_no, par, 0)
                rowmax(head_no, par, 1)
                invert(head_no, par, 0)
                invert(head_no, par, 1)
                rowmax(head_no, par, 2)
                invert(head_no, par, 2)
                rotate_mul_cos(0, head_no + 2)
                rowmax(head_no, par, 3)
                rotate_mul_sin(0)
                invert(head_no, par, 3)
                rowmax(head_no, par, 4)
                invert(head_no, par, 4)
                copy_v(head_no * FILLS + F_V, F_V, par, nxt)
                rotate_mul_cos(1, head_no + 2)
                rowmax(head_no, par, 5)
                rotate_mul_sin(1)
                invert(head_no, par, 5)
                split_lo(0, nxt, head_no * 2 + 3)
                split_lo(1, nxt, head_no * 2 + 4)

            with dve.Fori(0, B) as b:
                with dve.Fori(0, H // 2) as pair:
                    for par in range(2):
                        head(b * H + pair * 2 + par, par)

        @block.tensor
        def _(pe):
            pe.wait_ge(consts, 7)

            def project_qk(which, w_par, fill, par):
                hi, lo = ((WQ_HI, WQ_LO), (WK_HI, WK_LO))[which]
                for c in range(2):
                    cols = slice(c * BANK, (c + 1) * BANK)
                    last = matmul_split(pe, slot(fill, par)[:, cols], w_in[w_par][:, hi, :], w_in[w_par][:, lo, :],
                                        x_in[w_par][:, 0, cols], x_in[w_par][:, 1, cols], True, True)
                last.then_inc(filled, 1)

            def project_v(w_par, fill, par):
                for t in range(NT):
                    cols = slice(t * P, (t + 1) * P)
                    last = pe.matmul(slot(fill, par)[:, cols], xw_in[w_par][:, cols], wvo_in[w_par][:, :],
                                     start=True, stop=True)
                last.then_inc(filled, 1)

            def scores(of_par, slot_no, fill, par):
                q, k = qk[of_par]
                for i, t in enumerate(SLOT_TILES[slot_no]):
                    rows = slice(t * P, (t + 1) * P)
                    for c0 in range(0, width[t], BANK):
                        n = min(BANK, width[t] - c0)
                        out = slot(fill, par)[:, i * BANK + c0:i * BANK + c0 + n]
                        pe.matmul(out, q[:, 0, rows], k[:, 0, c0:c0 + n], start=True, stop=False,
                                  skip_group_check=True)
                        if c0 + n == width[t]:
                            pe.matmul(out[:, n - P:n], ident_b[:, :], mask_b[:, :], start=False, stop=False,
                                      skip_group_check=True)
                        pe.matmul(out, q[:, 0, rows], k[:, 1, c0:c0 + n], start=False, stop=False,
                                  skip_group_check=True)
                        last = pe.matmul(out, q[:, 1, rows], k[:, 0, c0:c0 + n], start=False, stop=True,
                                         skip_group_check=True)
                last.then_inc(filled, 1)

            def turn(head_no, par, slot_no):
                c = max(stat_col[t] for t in SLOT_TILES[slot_no])
                pe.wait_ge(normed, head_no * NT + c + 1)
                for bank_no, (from_slot, parts) in enumerate(TURN_BANKS):
                    if from_slot != slot_no:
                        continue
                    pe.wait_ge(turn_copied, head_no * NB_TURN + bank_no + 1)
                    bank, at = (bank_no + par * NB_TURN) % 2, 0
                    for t, j0, j1 in parts:
                        for j in range(j0, j1):
                            last = pe.transpose(ps_turn[:, bank, at:at + P],
                                                probs[:, p_at[t] + j * P:p_at[t] + (j + 1) * P], ident[:, :])
                            at += P
                    last.then_inc(turned, 1)

            def weigh(par, g, j_first, j_end):
                for j in range(j_first, j_end):
                    c0 = max(0, j - 4 * g) * P
                    last = pe.matmul(ps_y[:, g, c0:BANK], v_in[par][:, j * P:(j + 1) * P], pt[g][:, j, c0:BANK],
                                     start=False, stop=False, skip_group_check=True)
                return last

            def zero_y():
                for g in range(2):
                    pe.matmul(ps_y[:, g, :], zeros_b[:, 0:P], zeros_b[:, :], start=True, stop=False,
                              skip_group_check=True)

            pe.wait_ge(w_landed[0], 32)
            pe.wait_ge(x_landed[0], 32)
            project_qk(0, 0, 1, 0)
            project_qk(1, 0, 2, 0)
            pe.wait_ge(qk_raw, 1)
            project_v(0, F_V0, 0)
            pe.wait_ge(qk_lo, 2)
            scores(0, 0, F_S7, 0)
            pe.wait_ge(v_copied, 1)
            scores(0, 1, F_S6, 0)
            zero_y()

            def head(head_no, par, inputs):
                nxt = 1 - par
                pe.wait_ge(w_landed[nxt], inputs)
                pe.wait_ge(x_landed[nxt], inputs)
                pe.wait_ge(exped, head_no * 6 + 1)
                project_qk(0, nxt, F_Q, par)
                turn(head_no, par, 0)
                pe.wait_ge(exped, head_no * 6 + 2)
                scores(par, 2, F_S5, par)
                turn(head_no, par, 1)
                pe.wait_ge(qk_raw, head_no * 2 + 3)
                project_qk(1, nxt, F_K, par)
                pe.wait_ge(exped, head_no * 6 + 3)
                scores(par, 3, F_S4, par)
                turn(head_no, par, 2)
                pe.wait_ge(qk_raw, head_no * 2 + 4)
                scores(par, 4, F_S32, par)
                pe.wait_ge(exped, head_no * 6 + 4)
                project_v(nxt, F_V, par)
                turn(head_no, par, 3)
                pe.wait_ge(exped, head_no * 6 + 5)
                scores(par, 5, F_S10, par)
                pe.wait_ge(turn_copied, head_no * NB_TURN + 2 + BANKS_HIGH)
                weigh(par, 1, 0, 4)
                turn(head_no, par, 4)
                turn(head_no, par, 5)
                weigh(par, 1, 4, 8)
                pe.wait_ge(qk_lo, head_no * 2 + 4)
                pe.wait_ge(v_copied, head_no + 2)
                scores(nxt, 0, F_S7_NEXT, par)
                pe.wait_ge(exped, head_no * 6 + 6)
                scores(nxt, 1, F_S6_NEXT, par)
                pe.wait_ge(turn_copied, head_no * NB_TURN + 2 + NB_TURN)
                weigh(par, 0, 0, 4).then_inc(pv_done, 1)

            with pe.Fori(0, B) as b:
                with pe.Fori(0, H // 2) as pair:
                    heads = b * H + pair * 2
                    loads = b * (H // 2) + pair
                    head(heads, 0, loads * 32 + 32)
                    head(heads + 1, 1, loads * 32 + 64)
                pe.wait_ge(y_copied, b + 1)
                zero_y()


def ffn_block(nc, x, y_t, gamma_x, gamma_slot, slots, w1, w2, out):
    B, T, D = x.shape
    N = slots.shape[0] * slots.shape[1]
    F = w1.shape[1]
    NT, NC, FC = T // P, N // P, F // P
    assert D == P and N == BANK and F == BANK and NT == 8 and B % 2 == 0

    with ExitStack() as ctx:
        s = Scope(nc, ctx)
        y_in = s.sb("y_in", [P, T], F32)
        x_row = s.sb("x_row1", [P, NT, D], F32)
        res = s.sb("res", [P, NT, D], F32)
        x1 = [s.sb(f"x1_{i}", [P, NT, D], F32) for i in range(2)]
        z_row = s.sb("z_row", [P, NT, D], F32)
        z = s.sb("z", [P, 2, NT, D], F32R)
        z_t = s.sb("z_t", [P, 2, T], F32R)
        rows_n = s.sb("rows_n", [P, 2, T], F32)
        rows_s = s.sb("rows_s", [P, 4, N], F32)
        disp = s.sb("disp", [P, 2, NT, N], F32R)
        comb = s.sb("comb", [P, 2, NC, T], F32R)
        slot_in = s.sb("slot_in", [P, 2, N], F32R)
        hid = s.sb("hid", [P, FC, N], F32)
        hid_s = s.sb("hid_s", [P, 2, FC, N], F32R)
        proc = s.sb("proc", [P, 2, NC * D], F32R)
        o_t = s.sb("o_t", [P, T], F32)
        res2 = s.sb("res2", [P, NT, D], F32)
        out_row = s.sb("out_row", [P, NT, D], F32)
        stats = s.sb("stats", [P, 2, NT, 6], F32)
        mv = s.sb("mv", [P, 2, NT, 2], F32)
        neg_mean = s.sb("neg_mean", [P, 2, NT], F32)
        rstd = s.sb("rstd", [P, 2, NT], F32)
        power = s.sb("power", [P, 2, NT], F32)
        rms = s.sb("rms", [P, NT], F32)
        minus_half = s.sb("minus_half", [P, NT], F32)
        neg_max = s.sb("neg_max1", [P, 4 + NT], F32)
        sums = s.sb("sums1", [P, 4 + NT], F32)
        inv = s.sb("inv1", [P, 4 + NT], F32)
        ident = s.sb("ident2", [P, P], F32)
        gammas = s.sb("gammas", [P, 2], F32)
        gamma_both = s.sb("gamma_both", [P, 1], F32)
        w1_raw = s.sb("w1_raw", [P, F], F32)
        w2_raw = s.sb("w2_raw", [P, FC, D], F32)
        w1_s = s.sb("w1_s", [P, 2, F], F32R)
        w2_s = s.sb("w2_s", [P, 2, FC, D], F32R)
        se_raw = s.sb("se_raw", [P, NC, D], F32)
        se_sq = s.sb("se_sq", [P, NC, D], F32)
        se_row = s.sb("se_row", [P, NC, D], F32)
        se_t = s.sb("se_t", [P, 2, N], F32R)
        ps_slot = s.ps("ps_slot1", [P, 2, T])
        ps_turn = s.ps("ps_turn1", [P, 2, BANK])
        ps_acc = s.ps("ps_acc", [P, 2, BANK])

        w_landed, in_landed = s.sem("w_landed1"), s.sem("in_landed_f")
        consts, setup, se_norm = s.sem("consts1"), s.sem("setup"), s.sem("se_norm")
        ticks, dve_ticks = s.sem("ticks1"), s.sem("dve_ticks")
        filled, turned = s.sem("filled1"), s.sem("turned1")
        slots_summed, proc_summed = s.sem("slots_summed"), s.sem("proc_summed")
        maxed, inverted = s.sem("maxed1"), s.sem("inverted1")
        added = s.sem("added")
        stats_a, stats_b = s.sem("stats_a"), s.sem("stats_b")
        turn_lo, zt_lo, z_lo = s.sem("turn_lo1"), s.sem("zt_lo"), s.sem("z_lo")
        slot_in_hi, slot_in_lo = s.sem("slot_in_hi"), s.sem("slot_in_lo")
        hid_lo, proc_lo = s.sem("hid_lo"), s.sem("proc_lo")
        exped, turn_hi = s.sem("exped1"), s.sem("turn_hi1")
        zt_hi, z_hi, gelued, hid_hi = s.sem("zt_hi"), s.sem("z_hi"), s.sem("gelued"), s.sem("hid_hi")
        proc_hi, o_copied = s.sem("proc_hi"), s.sem("o_copied")
        normed = s.sem("normed1")
        ln_step, z_made, o_stats = s.sem("ln_step"), s.sem("z_made"), s.sem("o_stats")
        out_made, out_free = s.sem("out_made"), s.sem("out_free")

        ROW_SLOTS = ((0,), (1,), (2,), (3,), (4, 5), (6, 7), (8, 9), (10, 11))
        FILLS = 14
        F_ROWS = (3, 4, 5, 6, 7, 8, 9, 10)
        F_H01, F_H23, F_A1, F_OUT, F_BACK, F_A2 = range(11, 17)

        def slot(fill):
            return ps_slot[:, (fill - 1) % 2, :]

        def row_tile(i, fill):
            if i < 4:
                return slot(fill), rows_n[:, i % 2, :]
            return slot(fill)[:, (i % 2) * BANK:(i % 2 + 1) * BANK], rows_s[:, i % 4, :]

        def turn_view(bank_no, part):
            src = ps_turn[:, bank_no % 2, :].rearrange("p (j c) -> p j c", c=P)
            if bank_no < 8:
                c, half = bank_no // 2, bank_no % 2
                return disp[:, part, 4 * half:4 * half + 4, c * P:(c + 1) * P], src
            t = bank_no - 8
            return comb[:, part, :, t * P:(t + 1) * P], src

        block = ctx.enter_context(nc.Block())

        @block.sync
        def _(sp):
            def load(b):
                sp.dma_start(y_in[:, :], y_t[b, :, :]).then_inc(in_landed, 16)
                sp.dma_start(x_row[:, :, :], x[b, :, :].rearrange("(t p) m -> p t m", p=P)).then_inc(in_landed, 16)

            sp.dma_start(gammas[:, 0:1], gamma_x.rearrange("(p a) -> p a", a=1)).then_inc(w_landed, 16)
            sp.dma_start(gammas[:, 1:2], gamma_slot.rearrange("(p a) -> p a", a=1)).then_inc(w_landed, 16)
            sp.dma_start(se_raw[:, :, :], slots.rearrange("e t d -> (e t) d").rearrange("(c p) d -> p c d", p=P))\
              .then_inc(w_landed, 16)
            load(0)
            sp.dma_start(w1_raw[:, :], w1).then_inc(w_landed, 16)
            sp.dma_start(w2_raw[:, :, :], w2.rearrange("(c p) d -> p c d", p=P)).then_inc(w_landed, 16)

            def batch(b, ahead):
                if ahead:
                    sp.wait_ge(added, b * 2 + 1)
                    load(b + 1)
                sp.wait_ge(out_made, b * NT + NT)
                sp.dma_start(out[b, :, :].rearrange("(t p) m -> p t m", p=P), out_row[:, :, :])\
                  .then_inc(out_free, 16)

            with sp.Fori(0, B - 1) as b:
                batch(b, True)
            batch(B - 1, False)
            sp.wait_ge(out_free, 16 * B + 1)

        @block.gpsimd
        def _(pool):
            pool.memset(ident[:, :], 0.0).then_inc(consts, 1)
            pool.memset(minus_half[:, :], -0.5).then_inc(consts, 1)
            pool.memset(out_row[:, :, :], 0.0).then_inc(out_free, 1)
            pool.wait_ge(consts, 2)
            pool.affine_select(out=ident[:, :], in_=ident[:, :], compare_op=ALU.not_equal, fill=1.0,
                               base=0, pattern=[[-1, P]], channel_multiplier=1).then_inc(consts, 1)

            class Steps:
                at = 0

            def step(ins, base):
                Steps.at += 1
                ins.then_inc(ln_step, 1)
                wait_apart(pool, ln_step, base + Steps.at, ticks)

            def mean_rstd(which, base):
                step(pool.tensor_scalar(neg_mean[:, which, :], mv[:, which, :, 0], -1.0, 1.0, ALU.mult, ALU.mult), base)
                step(pool.tensor_scalar(power[:, which, :], mv[:, which, :, 1], LN_EPS, 1.0, ALU.add, ALU.mult), base)
                step(pool.tensor_tensor(rstd[:, which, :], power[:, which, :], minus_half[:, :], ALU.pow), base)

            def first_norm(par, stats_count, base):
                wait_apart(pool, stats_b, stats_count, ticks)
                mean_rstd(0, base)
                step(pool.tensor_tensor(rms[:, :], mv[:, 0, :, 1], rstd[:, 0, :], ALU.mult), base)
                step(pool.tensor_tensor(rms[:, :], rms[:, :], rstd[:, 0, :], ALU.mult), base)
                step(pool.tensor_scalar(rms[:, :], rms[:, :], float(D), 1e-24, ALU.mult, ALU.max), base)
                step(pool.tensor_tensor(rms[:, :], rms[:, :], minus_half[:, :], ALU.pow), base)
                for t in range(NT):
                    last = pool.tensor_scalar(x1[par][:, t, :], res[:, t, :], neg_mean[:, 0, t:t + 1],
                                              rstd[:, 0, t:t + 1], ALU.add, ALU.mult)
                step(last, base)
                for t in range(NT):
                    pool.tensor_scalar(z_row[:, t, :], x1[par][:, t, :], rms[:, t:t + 1], float(D) ** 0.5,
                                       ALU.mult, ALU.mult).then_inc(z_made, 1)

            def norm_rows(b, i):
                wait_apart(pool, inverted, b * 12 + i + 1, ticks)
                _, row = row_tile(i, 1)
                pool.tensor_scalar(row, row, inv[:, i:i + 1], 1.0, ALU.mult, ALU.mult).then_inc(normed, 1)

            pool.wait_ge(setup, NC)
            step(pool.tensor_scalar(rms[:, 0:NC], rms[:, 0:NC], 1e-24, 1.0, ALU.max, ALU.mult), 0)
            step(pool.tensor_tensor(rms[:, 0:NC], rms[:, 0:NC], minus_half[:, 0:NC], ALU.pow), 0)
            for c in range(NC):
                last = pool.tensor_scalar(se_row[:, c, :], se_raw[:, c, :], rms[:, c:c + 1], float(D) ** 0.5,
                                          ALU.mult, ALU.mult)
            last.then_inc(se_norm, 1)
            pool.wait_ge(se_norm, 1)
            first_norm(0, 1, 0)
            ahead_of_loop = Steps.at
            per_batch = 3 + 8

            def batch(b, par, ahead):
                Steps.at = ahead_of_loop
                base = b * per_batch
                for i in range(12):
                    norm_rows(b, i)
                if ahead:
                    first_norm(1 - par, b + 2, base)
                wait_apart(pool, o_stats, b + 1, ticks)
                mean_rstd(1, base)
                wait_apart(pool, out_free, b * 16 + 1, ticks)
                for t in range(NT):
                    pool.tensor_scalar(out_row[:, t, :], res2[:, t, :], neg_mean[:, 1, t:t + 1],
                                       rstd[:, 1, t:t + 1], ALU.add, ALU.mult).then_inc(out_made, 1)

            with pool.Fori(0, B // 2 - 1) as pair:
                for par in range(2):
                    batch(pair * 2 + par, par, True)
            batch(B - 2, 0, True)
            batch(B - 1, 1, False)

        @block.scalar
        def _(act):
            def exp(b, k):
                for i in ROW_SLOTS[k]:
                    act.wait_ge(maxed, b * 12 + i + 1)
                    src, row = row_tile(i, F_ROWS[k])
                    last = act.activation(row, src, ACT.Exp, bias=neg_max[:, i:i + 1], accum_out=sums[:, i:i + 1])
                last.then_inc(exped, 1)

            def split_turn(b, bank_no):
                act.wait_ge(turned, b * 16 + bank_no + 2)
                dst, src = turn_view(bank_no, 0)
                act.activation(dst, src, ACT.Copy).then_inc(turn_hi, 1)

            def split_z(count):
                act.wait_ge(z_made, count * NT)
                act.activation(z[:, 0, :, :], z_row[:, :, :], ACT.Copy).then_inc(z_hi, 1)

            def split_zt(fill_no, fill):
                act.wait_ge(filled, fill_no)
                act.activation(z_t[:, 0, :], slot(fill), ACT.Copy).then_inc(zt_hi, 1)

            split_z(1)
            split_zt(2, 2)

            def batch(b, ahead):
                exp(b, 0)
                exp(b, 1)
                split_turn(b, 0)
                split_turn(b, 1)
                exp(b, 2)
                split_turn(b, 2)
                split_turn(b, 3)
                exp(b, 3)
                split_turn(b, 4)
                split_turn(b, 5)
                exp(b, 4)
                split_turn(b, 6)
                split_turn(b, 7)
                exp(b, 5)
                split_turn(b, 8)
                split_turn(b, 9)
                exp(b, 6)
                split_turn(b, 10)
                split_turn(b, 11)
                exp(b, 7)
                split_turn(b, 12)
                split_turn(b, 13)
                for c in range(FC):
                    fill = (F_H01, F_H23)[c // 2]
                    if c % 2 == 0:
                        act.wait_ge(filled, b * FILLS + fill)
                    act.activation(hid[:, c, :], slot(fill)[:, (c % 2) * BANK:(c % 2 + 1) * BANK],
                                   ACT.Gelu).then_inc(gelued, 1)
                for c in range(FC):
                    act.wait_ge(gelued, b * FC + c + 1)
                    act.activation(hid_s[:, 0, c, :], hid[:, c, :], ACT.Copy).then_inc(hid_hi, 1)
                split_turn(b, 14)
                split_turn(b, 15)
                act.wait_ge(proc_summed, b + 1)
                act.activation(proc[:, 0, :], ps_acc[:, 1, :], ACT.Copy).then_inc(proc_hi, 1)
                act.wait_ge(filled, b * FILLS + F_OUT - (0 if ahead else 1))
                act.activation(o_t[:, :], slot(F_OUT), ACT.Copy).then_inc(o_copied, 1)
                if ahead:
                    split_z(b + 2)
                    split_zt(b * FILLS + F_A2, F_A2)

            with act.Fori(0, B - 1) as b:
                batch(b, True)
            batch(B - 1, False)

        @block.vector
        def _(dve):
            dve.wait_ge(w_landed, 80)
            for c in range(NC):
                dve.tensor_tensor_reduce(se_sq[:, c, :], se_raw[:, c, :], se_raw[:, c, :], 1.0, 0.0,
                                         ALU.mult, ALU.add, rms[:, c:c + 1]).then_inc(setup, 1)
            dve.tensor_tensor(gamma_both[:, :], gammas[:, 0:1], gammas[:, 1:2], ALU.mult).then_inc(setup, 1)
            dve.tensor_copy(w1_s[:, 0, :], w1_raw[:, :]).then_inc(setup, 1)
            dve.tensor_copy(w2_s[:, 0, :, :], w2_raw[:, :, :]).then_inc(setup, 1)
            dve.wait_ge(setup, NC + 3)
            dve.tensor_tensor(w1_s[:, 1, :], w1_raw[:, :], f32(w1_s[:, 0, :]), ALU.subtract).then_inc(setup, 1)
            dve.tensor_tensor(w2_s[:, 1, :, :], w2_raw[:, :, :], f32(w2_s[:, 0, :, :]), ALU.subtract)\
               .then_inc(setup, 1)
            dve.wait_ge(turned, 1)
            dve.tensor_scalar(se_t[:, 0, :], ps_turn[:, 0, :], gamma_both[:, 0:1], None, ALU.mult).then_inc(setup, 1)
            dve.wait_ge(setup, NC + 6)
            dve.scalar_tensor_tensor(se_t[:, 1, :], ps_turn[:, 0, :], gamma_both[:, 0:1], f32(se_t[:, 0, :]),
                                     ALU.mult, ALU.subtract).then_inc(turn_lo, 1)
            dve.memset(neg_max[:, :], 0.0).then_inc(turn_lo, 1)
            dve.wait_ge(turn_lo, 2)

            def add_stats(fill_no, fill, other, dst, which, stats_count, done):
                dve.wait_ge(filled, fill_no)
                dve.tensor_tensor(dst[:, :, :], slot(fill).rearrange("p (t m) -> p t m", m=D), other[:, :, :],
                                  ALU.add).then_inc(added, 1)
                dve.wait_ge(added, stats_count)
                for t in range(NT):
                    last = dve.bn_stats(stats[:, which, t, :], dst[:, t, :])
                last.then_inc(stats_a, 1)
                wait_apart(dve, stats_a, stats_count, dve_ticks)
                for t in range(NT):
                    last = dve.bn_aggr(mv[:, which, t, :], stats[:, which, t, :])
                last.then_inc(done, 1)

            def split_zt(count, fill):
                dve.wait_ge(zt_hi, count)
                dve.tensor_tensor(z_t[:, 1, :], slot(fill), f32(z_t[:, 0, :]), ALU.subtract).then_inc(zt_lo, 1)

            def split_z(count):
                dve.wait_ge(z_hi, count)
                dve.tensor_tensor(z[:, 1, :, :], z_row[:, :, :], f32(z[:, 0, :, :]), ALU.subtract).then_inc(z_lo, 1)

            def rowmax(b, k):
                dve.wait_ge(filled, b * FILLS + F_ROWS[k])
                for i in ROW_SLOTS[k]:
                    src, _ = row_tile(i, F_ROWS[k])
                    dve.tensor_reduce(neg_max[:, i:i + 1], src, AX.X, ALU.max, negate=True).then_inc(maxed, 1)

            def invert(b, k):
                dve.wait_ge(exped, b * 8 + k + 1)
                for i in ROW_SLOTS[k]:
                    dve.reciprocal(inv[:, i:i + 1], sums[:, i:i + 1]).then_inc(inverted, 1)

            def split_turn(b, bank_no):
                dve.wait_ge(turn_hi, b * 16 + bank_no + 1)
                dst, src = turn_view(bank_no, 1)
                dve.tensor_tensor(dst, src, f32(turn_view(bank_no, 0)[0]), ALU.subtract).then_inc(turn_lo, 1)

            dve.wait_ge(in_landed, 32)
            add_stats(1, 1, x_row, res, 0, 1, stats_b)
            split_z(1)
            split_zt(1, 2)

            def batch(b, par, ahead):
                rowmax(b, 0)
                rowmax(b, 1)
                invert(b, 0)
                invert(b, 1)
                for k in range(2, 8):
                    rowmax(b, k)
                    split_turn(b, 2 * k - 4)
                    split_turn(b, 2 * k - 3)
                    invert(b, k)
                    if k == 6:
                        dve.wait_ge(slots_summed, b + 1)
                        dve.tensor_scalar(slot_in[:, 0, :], ps_acc[:, 0, :], gammas[:, 0:1], None,
                                          ALU.mult).then_inc(slot_in_hi, 1)
                        dve.wait_ge(slot_in_hi, b + 1)
                        dve.scalar_tensor_tensor(slot_in[:, 1, :], ps_acc[:, 0, :], gammas[:, 0:1],
                                                 f32(slot_in[:, 0, :]), ALU.mult, ALU.subtract).then_inc(slot_in_lo, 1)
                split_turn(b, 12)
                split_turn(b, 13)
                for c in range(FC):
                    dve.wait_ge(hid_hi, b * FC + c + 1)
                    dve.tensor_tensor(hid_s[:, 1, c, :], hid[:, c, :], f32(hid_s[:, 0, c, :]),
                                      ALU.subtract).then_inc(hid_lo, 1)
                split_turn(b, 14)
                split_turn(b, 15)
                if ahead:
                    dve.wait_ge(in_landed, b * 32 + 64)
                    add_stats(b * FILLS + F_A1, F_A1, x_row, res, 0, b * 2 + 2, stats_b)
                dve.wait_ge(proc_hi, b + 1)
                dve.tensor_tensor(proc[:, 1, :], ps_acc[:, 1, :], f32(proc[:, 0, :]), ALU.subtract).then_inc(proc_lo, 1)
                add_stats(b * FILLS + F_BACK - (0 if ahead else 1), F_BACK, x1[par], res2, 1,
                          b * 2 + (3 if ahead else 2), o_stats)
                if ahead:
                    split_z(b + 2)
                    split_zt(b + 2, F_A2)

            with dve.Fori(0, B // 2 - 1) as pair:
                for par in range(2):
                    batch(pair * 2 + par, par, True)
            batch(B - 2, 0, True)
            batch(B - 1, 1, False)

        @block.tensor
        def _(pe):
            pe.wait_ge(consts, 3)

            def transposes(src, fill):
                for t in range(NT):
                    last = pe.transpose(slot(fill)[:, t * P:(t + 1) * P], src(t), ident[:, :])
                last.then_inc(filled, 1)

            def rows(k):
                for i in ROW_SLOTS[k]:
                    dst, _ = row_tile(i, F_ROWS[k])
                    if i < 4:
                        own = slice(i * P, (i + 1) * P)
                        for c in range(2):
                            cols = slice(c * BANK, (c + 1) * BANK)
                            last = matmul_split(pe, dst[:, cols], se_t[:, 0, own], se_t[:, 1, own],
                                                z_t[:, 0, cols], z_t[:, 1, cols], True, True)
                    else:
                        own = slice((i - 4) * P, (i - 3) * P)
                        last = matmul_split(pe, dst, z_t[:, 0, own], z_t[:, 1, own],
                                            se_t[:, 0, :], se_t[:, 1, :], True, True)
                last.then_inc(filled, 1)

            def turn(b, k):
                for n, i in enumerate(ROW_SLOTS[k]):
                    pe.wait_ge(normed, b * 12 + i + 1)
                    _, row = row_tile(i, 1)
                    for half in range(len(ROW_SLOTS[k]) % 2 + 1):
                        bank_no = 2 * k + n + half
                        pe.wait_ge(turn_lo, b * 16 + bank_no + 1)
                        for j in range(4):
                            last = pe.transpose(ps_turn[:, bank_no % 2, j * P:(j + 1) * P],
                                                row[:, (4 * half + j) * P:(4 * half + j + 1) * P], ident[:, :])
                        last.then_inc(turned, 1)

            pe.wait_ge(in_landed, 32)
            transposes(lambda t: y_in[:, t * P:(t + 1) * P], 1)
            pe.wait_ge(se_norm, 1)
            for c in range(NC):
                last = pe.transpose(ps_turn[:, 0, c * P:(c + 1) * P], se_row[:, c, :], ident[:, :])
            last.then_inc(turned, 1)
            pe.wait_ge(z_made, NT)
            transposes(lambda t: z_row[:, t, :], 2)

            def batch(b, ahead):
                pe.wait_ge(zt_lo, b + 1)
                pe.wait_ge(added, b * 2 + 1)
                rows(0)
                rows(1)
                turn(b, 0)
                for k in range(2, 6):
                    pe.wait_ge(exped, b * 8 + k - 1)
                    rows(k)
                    turn(b, k - 1)
                pe.wait_ge(turn_lo, b * 16 + 8 + 2)
                pe.wait_ge(z_lo, b + 1)
                for t in range(NT):
                    last = matmul_split(pe, ps_acc[:, 0, :], z[:, 0, t, :], z[:, 1, t, :],
                                        disp[:, 0, t, :], disp[:, 1, t, :], t == 0, t == NT - 1)
                last.then_inc(slots_summed, 1)
                for k in range(6, 8):
                    pe.wait_ge(exped, b * 8 + k - 1)
                    rows(k)
                    turn(b, k - 1)
                for c in range(FC):
                    fill = (F_H01, F_H23)[c // 2]
                    if c % 2 == 0:
                        pe.wait_ge(exped, b * 8 + 7 + c // 2)
                    if c == 0:
                        pe.wait_ge(slot_in_lo, b + 1)
                    own = slice(c * P, (c + 1) * P)
                    last = matmul_split(pe, slot(fill)[:, (c % 2) * BANK:(c % 2 + 1) * BANK],
                                        w1_s[:, 0, own], w1_s[:, 1, own], slot_in[:, 0, :], slot_in[:, 1, :],
                                        True, True)
                    if c % 2 == 1:
                        last.then_inc(filled, 1)
                turn(b, 7)
                if ahead:
                    pe.wait_ge(in_landed, b * 32 + 64)
                    pe.wait_ge(gelued, b * FC + 2)
                    transposes(lambda t: y_in[:, t * P:(t + 1) * P], F_A1)
                pe.wait_ge(hid_lo, b * FC + FC)
                for n in range(NC):
                    own = slice(n * P, (n + 1) * P)
                    for c in range(FC):
                        last = matmul_split(pe, ps_acc[:, 1, own], hid_s[:, 0, c, own], hid_s[:, 1, c, own],
                                            w2_s[:, 0, c, :], w2_s[:, 1, c, :], c == 0, c == FC - 1)
                last.then_inc(proc_summed, 1)
                pe.wait_ge(proc_lo, b + 1)
                pe.wait_ge(turn_lo, b * 16 + 16 + 2)
                pe.wait_ge(gelued, b * FC + FC)
                for h in range(2):
                    cols = slice(h * BANK, (h + 1) * BANK)
                    for c in range(NC):
                        own = slice(c * P, (c + 1) * P)
                        last = matmul_split(pe, slot(F_OUT)[:, cols], proc[:, 0, own], proc[:, 1, own],
                                            comb[:, 0, c, cols], comb[:, 1, c, cols], c == 0, c == NC - 1)
                last.then_inc(filled, 1)
                pe.wait_ge(o_copied, b + 1)
                if ahead:
                    pe.wait_ge(added, b * 2 + 2)
                transposes(lambda t: o_t[:, t * P:(t + 1) * P], F_BACK)
                if ahead:
                    pe.wait_ge(z_made, b * NT + 2 * NT)
                    transposes(lambda t: z_row[:, t, :], F_A2)

            with pe.Fori(0, B - 1) as b:
                batch(b, True)
            batch(B - 1, False)


def build(nc, x, wq, wk, wv, wo, gamma_x, gamma_slot, slots, w1, w2, rope_c, rope_s, out):
    B, T, M = x.shape
    H = wq.shape[1]
    w_split = nc.dram_tensor("w_split", (H, M, NW, P), F32, kind="Internal").ap()
    x_split = nc.dram_tensor("x_split", (B + 1, M, NX, T), F32, kind="Internal").ap()
    y_t = nc.dram_tensor("y_t", (B, M, T), F32, kind="Internal").ap()
    prepare_block(nc, x, wq, wk, wv, wo, w_split, x_split)
    attention_block(nc, w_split, x_split, rope_c, rope_s, y_t, B, H, T)
    ffn_block(nc, x, y_t, gamma_x, gamma_slot, slots, w1, w2, out)


_INS = ["L0_attn_x", "L0_attn_wq", "L0_attn_wk", "L0_attn_wv", "L0_attn_wo", "L0_ffn_gamma_x",
        "L0_ffn_gamma_slot", "L0_ffn_slot_embeds", "L0_ffn_w1", "L0_ffn_w2"]


def kernel(**inputs):
    import concourse.bacc as _bacc
    from concourse.bass_utils import run_bass_kernel_spmd as _run

    nc = _bacc.Bacc("TRN2", target_bir_lowering=False, num_devices=1)
    arrays = {f"in_{name}": np.ascontiguousarray(inputs[name]) for name in _INS}
    shape = arrays["in_L0_attn_x"].shape
    arrays["rope_c"], arrays["rope_s"] = rope_tables(shape[1], inputs["L0_attn_wq"].shape[2])
    args = [nc.dram_tensor(n, a.shape, mybir.dt.from_np(a.dtype), kind="ExternalInput").ap()
            for n, a in arrays.items()]
    out = nc.dram_tensor("out_0", shape, F32, kind="ExternalOutput").ap()
    build(nc, *args, out)
    r = _run(nc, [arrays], core_ids=[0])
    return r.results[0]["out_0"]
```

```python
from contextlib import ExitStack

import numpy as np

import concourse.bass as bass
from concourse import mybir

P = 128
BANK = 512
ALU = mybir.AluOpType
ACT = mybir.ActivationFunctionType
AX = mybir.AxisListType
F32 = mybir.dt.float32
F32R = mybir.dt.float32r
BF16 = mybir.dt.bfloat16
ROTARY_BASE = 10000.0
MASKED = -1e30
LN_EPS = 1e-5

WQ_HI, WQ_LO, WK_HI, WK_LO = range(4)


class Scope:

    def __init__(self, nc, ctx):
        self.nc, self.ctx = nc, ctx

    def sb(self, name, shape, dt):
        return self.ctx.enter_context(self.nc.sbuf_tensor(name, shape, dt))

    def ps(self, name, shape):
        return self.ctx.enter_context(self.nc.psum_tensor(name, shape, F32))

    def sem(self, name):
        return self.ctx.enter_context(self.nc.semaphore(name))


def matmul_split(pe, out, stat_hi, stat_lo, mov_hi, mov_lo, start, stop):
    pe.matmul(out, stat_hi, mov_hi, start=start, stop=False, skip_group_check=True)
    pe.matmul(out, stat_hi, mov_lo, start=False, stop=False, skip_group_check=True)
    return pe.matmul(out, stat_lo, mov_hi, start=False, stop=stop, skip_group_check=True)


def wait_apart(eng, sem, value, ticks):
    eng.wait_ge(sem, value)
    eng.sem_inc(ticks, 1)


def f32(ap):
    return ap.bitcast(F32)


class Kept:

    def __init__(self, s, H, T):
        self.w = s.sb("w_all", [P, H, 4, P], F32R)
        self.wvo = s.sb("wvo_all", [P, H, P], F32)
        self.x_rows = s.sb("x_rows", [P, T // P, P], F32)
        self.x_t = s.sb("x_t", [P, 2, T], F32R)
        self.x_whole = s.sb("x_whole", [P, T], F32)
        self.rope = s.sb("rope", [P, 2, T], F32)


def prepare_block(nc, x, wq, wk, wv, wo, rope_c, rope_s, kept):
    B, T, M = x.shape
    H = wq.shape[1]
    NT = T // P
    with ExitStack() as ctx:
        s = Scope(nc, ctx)
        w_raw = s.sb("w_raw", [P, 4, H * P], F32)
        wv_t = s.sb("wv_t", [P, H, P], F32)
        ident = s.sb("ident0", [P, P], F32)
        ps_w = s.ps("ps_w", [P, 2, H * P])
        ps_x = s.ps("ps_x", [P, T])
        ident_made = s.sem("ident_made0")
        x_landed, w_landed = s.sem("x_landed"), [s.sem(f"w_landed_{n}") for n in ("q", "k", "v", "o")]
        qk_split, rope_landed = s.sem("qk_split"), s.sem("rope_landed")
        wv_turned, wv_copied = s.sem("wv_turned"), s.sem("wv_copied")
        wvo_made, wvo_copied = s.sem("wvo_made"), s.sem("wvo_copied")
        x_turned, x_hi, x_lo, x_copied = s.sem("x_turned"), s.sem("x_hi"), s.sem("x_lo"), s.sem("x_copied")

        block = ctx.enter_context(nc.Block())

        @block.sync
        def _(sp):
            sp.dma_start(kept.x_rows[:, :, :], x[0, :, :].rearrange("(t p) m -> p t m", p=P)).then_inc(x_landed, 16)
            for i, w in ((0, wq), (2, wv)):
                sp.dma_start(w_raw[:, i, :], w.rearrange("m h d -> m (h d)")).then_inc(w_landed[i], 16)
            for i, table in enumerate((rope_c, rope_s)):
                sp.dma_start(kept.rope[:, i, :], table).then_inc(rope_landed, 16)
            sp.wait_ge(rope_landed, 32)

        @block.gpsimd
        def _(pool):
            pool.memset(ident[:, :], 0.0).then_inc(ident_made, 1)
            pool.wait_ge(ident_made, 1)
            pool.affine_select(out=ident[:, :], in_=ident[:, :], compare_op=ALU.not_equal, fill=1.0,
                               base=0, pattern=[[-1, P]], channel_multiplier=1).then_inc(ident_made, 1)

        @block.scalar
        def _(act):
            act.dma_start(w_raw[:, 1, :], wk.rearrange("m h d -> m (h d)")).then_inc(w_landed[1], 16)
            act.dma_start(w_raw[:, 3, :].rearrange("p (h m) -> p h m", h=H),
                          wo.rearrange("h d m -> d h m")).then_inc(w_landed[3], 16)
            act.wait_ge(x_turned, 1)
            act.activation(kept.x_whole[:, :], ps_x[:, :], ACT.Copy).then_inc(x_copied, 1)
            act.wait_ge(x_copied, 1)
            act.activation(kept.x_t[:, 0, :], kept.x_whole[:, :], ACT.Copy).then_inc(x_hi, 1)
            act.wait_ge(wv_turned, 1)
            act.activation(wv_t[:, :, :], ps_w[:, 0, :].rearrange("p (h m) -> p h m", h=H),
                           ACT.Copy).then_inc(wv_copied, 1)
            act.wait_ge(wvo_made, 1)
            act.activation(kept.wvo[:, :, :], ps_w[:, 1, :].rearrange("p (h m) -> p h m", h=H),
                           ACT.Copy).then_inc(wvo_copied, 1)

        @block.vector
        def _(dve):
            for i, (hi, lo, scale) in enumerate(((WQ_HI, WQ_LO, 1.0 / P), (WK_HI, WK_LO, 1.0))):
                dve.wait_ge(w_landed[i], 16)
                raw = w_raw[:, i, :].rearrange("p (h d) -> p h d", h=H)
                dve.tensor_scalar(kept.w[:, :, hi, :], raw, scale, None, ALU.mult).then_inc(qk_split, 1)
                dve.wait_ge(qk_split, 2 * i + 1)
                dve.scalar_tensor_tensor(kept.w[:, :, lo, :], raw, scale, f32(kept.w[:, :, hi, :]),
                                         ALU.mult, ALU.subtract).then_inc(qk_split, 1)
                if i == 0:
                    dve.wait_ge(x_hi, 1)
                    dve.tensor_tensor(kept.x_t[:, 1, :], kept.x_whole[:, :], f32(kept.x_t[:, 0, :]),
                                      ALU.subtract).then_inc(x_lo, 1)

        @block.tensor
        def _(pe):
            pe.wait_ge(ident_made, 2)
            pe.wait_ge(x_landed, 16)
            for t in range(NT):
                last = pe.transpose(ps_x[:, t * P:(t + 1) * P], kept.x_rows[:, t, :], ident[:, :])
            last.then_inc(x_turned, 1)
            pe.wait_ge(w_landed[2], 16)
            for h in range(H):
                last = pe.transpose(ps_w[:, 0, h * P:(h + 1) * P], w_raw[:, 2, h * P:(h + 1) * P], ident[:, :])
            last.then_inc(wv_turned, 1)
            pe.wait_ge(wv_copied, 1)
            pe.wait_ge(w_landed[3], 16)
            for h in range(H):
                last = pe.matmul(ps_w[:, 1, h * P:(h + 1) * P], wv_t[:, h, :],
                                 w_raw[:, 3, h * P:(h + 1) * P], start=True, stop=True)
            last.then_inc(wvo_made, 1)


def rope_tables(T, D):
    half = D // 2
    freq = np.power(np.float32(ROTARY_BASE), -np.arange(half, dtype=np.float32) / np.float32(half))
    ang = (np.arange(T, dtype=np.float32)[:, None] * freq.astype(np.float32)[None, :]).T
    cos, sin = np.cos(ang).astype(np.float32), np.sin(ang).astype(np.float32)
    return np.concatenate([cos, cos]), np.concatenate([-sin, sin])


SLOT_TILES = ((7,), (6,), (5,), (4,), (1, 0), (3, 2))
TILES = (7, 6, 5, 4, 1, 0, 3, 2)
TURN_BANKS = tuple(
    [(s, [(t, 0, 4)]) if half == 0 else (s, [(t, 4, t + 1)])
     for s, t in enumerate((7, 6, 5, 4)) for half in range(2)]
    + [(4, [(1, 0, 2), (0, 0, 1)]), (5, [(3, 0, 4)]), (5, [(2, 0, 3)])])
NB_TURN = len(TURN_BANKS)
BANKS_HIGH = 8
NB_SPLIT = 7
SPLIT_BANKS = (0, 2, 4, 6, 8, 9, 10)
FILLS = 9
F_V0 = 3
F_S7, F_S6, F_Q, F_K, F_S5, F_S4, F_V, F_S10, F_S32, F_S7_NEXT, F_S6_NEXT = range(4, 15)
SCORE_FILLS = (F_S7, F_S6, F_S5, F_S4, F_S10, F_S32)


def attention_block(nc, x, kept, y_t, B, H, T):
    NT = T // P
    D = P
    assert NT == 8 and H % 2 == 0
    width = {t: P * (t + 1) for t in TILES}
    p_at, at = {}, 0
    for t in TILES:
        p_at[t] = at
        at += width[t]
    stat_col = {t: i for i, t in enumerate(TILES)}
    K_ALL, Q_FIRST, Q_REST = range(3)
    PARTS = ((1, slice(0, T)), (0, slice(6 * P, T)), (0, slice(0, 6 * P)))

    with ExitStack() as ctx:
        s = Scope(nc, ctx)
        w_in = [s.sb(f"w_in{i}", [P, 4, D], F32R) for i in range(2)]
        wvo_in = [s.sb(f"wvo_in{i}", [P, D], F32) for i in range(2)]
        x_in = [s.sb(f"x_in{i}", [P, 2, T], F32R) for i in range(2)]
        xw_in = [s.sb(f"xw_in{i}", [P, T], F32) for i in range(2)]
        qk = [[s.sb(f"{n}{i}", [P, 2, T], F32R) for n in "qk"] for i in range(2)]
        v_low = [s.sb(f"v_low{i}", [P, 2, BANK], F32R) for i in range(2)]
        v_high = [s.sb(f"v_high{i}", [P, BANK], F32) for i in range(2)]
        unrot = [s.sb(f"unrot_{n}", [P, T], F32) for n in "qk"]
        rot = [s.sb(f"rot_{n}", [P, T], F32) for n in "qk"]
        swapped = [s.sb(f"swapped_{n}", [P, T], F32) for n in "qk"]
        probs = s.sb("probs", [P, at], F32)
        pt_low = s.sb("pt_low", [P, 2, 4, BANK], F32R)
        pt_split = s.sb("pt_split", [P, 2, 4, BANK], F32R)
        pt_high = s.sb("pt_high", [P, 4, BANK], F32)
        y_out = s.sb("y_out", [P, T], F32)
        neg_max = s.sb("neg_max", [P, 2, NT], F32)
        sums = s.sb("sums", [P, 2, NT], F32)
        inv = s.sb("inv", [P, 2, NT], F32)
        ident = s.sb("ident1", [P, P], F32)
        ident_b = s.sb("ident_b", [P, P], BF16)
        mask_b = s.sb("mask_b", [P, P], BF16)
        zeros_b = s.sb("zeros_b", [P, BANK], BF16)
        ps_slot = s.ps("ps_slot", [P, 2, T])
        ps_turn = s.ps("ps_turn", [P, 2, BANK])
        ps_y = s.ps("ps_y", [P, 2, BANK])

        consts, ticks = s.sem("consts"), s.sem("ticks")
        x_rows_landed, x_turned = s.sem("x_rows_landed"), s.sem("x_turned1")
        x_copied, x_hi, x_lo = s.sem("x_copied1"), s.sem("x_hi1"), s.sem("x_lo1")
        w_landed = [s.sem(f"w_landed{i}") for i in range(2)]
        x_landed = [s.sem(f"x_landed_a{i}") for i in range(2)]
        filled = s.sem("filled")
        turned = s.sem("turned")
        v_half = s.sem("v_half")
        pv_done = s.sem("pv_done")
        maxed = s.sem("maxed")
        inverted = s.sem("inverted")
        cos_made = [s.sem(f"cos_made_{n}") for n in "qk"]
        sin_made = [s.sem(f"sin_made_{n}") for n in "qk"]
        v_hi, v_lo, v_copied = s.sem("v_hi"), s.sem("v_lo"), s.sem("v_copied")
        turn_lo = s.sem("turn_lo")
        rotated = [s.sem(f"rotated_{n}") for n in ("k", "q_first", "q_rest")]
        hi_made = [s.sem(f"hi_made_{n}") for n in ("k", "q_first", "q_rest")]
        lo_made = [s.sem(f"lo_made_{n}") for n in ("k", "q_first", "q_rest")]
        exped = s.sem("exped")
        qk_raw, turn_copied = s.sem("qk_raw"), s.sem("turn_copied")
        y_copied, y_free = s.sem("y_copied"), s.sem("y_free")
        normed = s.sem("normed")
        swap_landed = [s.sem(f"swap_landed_{n}") for n in "qk"]

        def slot(fill, par):
            return ps_slot[:, (fill + par * FILLS - 1) % 2, :]

        def turn_views(bank_no, par, part=0):
            at = 0
            bank = (bank_no + par * NB_TURN) % 2
            for t, j0, j1 in TURN_BANKS[bank_no][1]:
                c = (t % 4) * P
                src = ps_turn[:, bank, at:at + (j1 - j0) * P].rearrange("p (j c) -> p j c", c=P)
                if t < 4:
                    yield pt_low[:, part, j0:j1, c:c + P], src
                elif j0 == 0:
                    yield pt_split[:, part, :, c:c + P], src
                else:
                    yield pt_high[:, j0 - 4:j1 - 4, c:c + P], src
                at += (j1 - j0) * P

        block = ctx.enter_context(nc.Block())

        @block.sync
        def _(sp):
            def load_w(head, par):
                sp.dma_start(f32(w_in[par][:, :, :]), f32(kept.w[:, head, :, :])).then_inc(w_landed[par], 16)
                sp.dma_start(wvo_in[par][:, :], kept.wvo[:, head, :]).then_inc(w_landed[par], 16)

            def load_x(par):
                sp.dma_start(f32(x_in[par][:, :, :]), f32(kept.x_t[:, :, :])).then_inc(x_landed[par], 16)
                sp.dma_start(xw_in[par][:, :], kept.x_whole[:, :]).then_inc(x_landed[par], 16)

            def load_x_rows(batch):
                sp.dma_start(kept.x_rows[:, :, :], x[batch, :, :].rearrange("(t p) m -> p t m", p=P))\
                  .then_inc(x_rows_landed, 16)

            def swap(which, raw_count):
                sp.wait_ge(qk_raw, raw_count)
                for half in range(2):
                    sp.dma_start(swapped[which][64 * half:64 * half + 64, :],
                                 unrot[which][64 - 64 * half:128 - 64 * half, :]).then_inc(swap_landed[which], 16)

            sp.sem_inc(w_landed[0], 32)
            swap(0, 1)
            swap(1, 2)
            load_x(0)
            load_w(1, 1)
            load_x(1)
            load_x_rows(1)

            def head(b, head_no, par, next_w, new_x):
                sp.wait_ge(filled, head_no * FILLS + F_S6)
                load_w(next_w, par)
                if new_x:
                    sp.wait_ge(x_lo, b + 1)
                    load_x(par)
                else:
                    sp.sem_inc(x_landed[par], 32)
                swap(0, head_no * 2 + 3)
                swap(1, head_no * 2 + 4)

            def batch(b, more):
                with sp.Fori(0, H // 2 - 1) as pair:
                    for par in range(2):
                        head(b, b * H + pair * 2 + par, par, pair * 2 + 2 + par, False)
                for par in range(2):
                    head(b, b * H + (H - 2 + par), par, par, True)
                sp.wait_ge(x_turned, b + 1)
                if more:
                    load_x_rows(b + 2)
                else:
                    sp.sem_inc(x_rows_landed, 16)
                sp.wait_ge(y_copied, b + 2)
                sp.dma_start(y_t[b, :, :], y_out[:, :]).then_inc(y_free, 16)

            with sp.Fori(0, B - 2) as b:
                batch(b, True)
            for b in range(B - 2, B):
                batch(b, False)
            sp.wait_ge(y_free, 16 * B + 1)
            for par in range(2):
                sp.wait_ge(w_landed[par], 32 * (B * H // 2 + 1))
                sp.wait_ge(x_landed[par], 32 * (B * H // 2 + 1))

        @block.gpsimd
        def _(pool):
            pool.memset(ident[:, :], 0.0).then_inc(consts, 1)
            pool.memset(ident_b[:, :], 0.0).then_inc(consts, 1)
            pool.memset(mask_b[:, :], 0.0).then_inc(consts, 1)
            pool.memset(zeros_b[:, :], 0.0).then_inc(consts, 1)
            pool.memset(y_out[:, :], 0.0).then_inc(y_free, 1)
            pool.wait_ge(consts, 4)
            for m in (ident, ident_b):
                pool.affine_select(out=m[:, :], in_=m[:, :], compare_op=ALU.not_equal, fill=1.0,
                                   base=0, pattern=[[-1, P]], channel_multiplier=1).then_inc(consts, 1)
            pool.affine_select(out=mask_b[:, :], in_=mask_b[:, :], compare_op=ALU.is_ge, fill=MASKED,
                               base=0, pattern=[[-1, P]], channel_multiplier=1).then_inc(consts, 1)

            def mul_cos_k(count):
                wait_apart(pool, qk_raw, count * 2, ticks)
                pool.tensor_tensor(rot[1][:, :], unrot[1][:, :], kept.rope[:, 0, :], ALU.mult).then_inc(cos_made[1], 1)

            def mul_sin(which, count):
                wait_apart(pool, swap_landed[which], count * 32, ticks)
                pool.tensor_tensor(swapped[which][:, :], swapped[which][:, :], kept.rope[:, 1, :],
                                   ALU.mult).then_inc(sin_made[which], 1)

            def norm(head_no, par, slot_no):
                wait_apart(pool, inverted, head_no * 6 + slot_no + 1, ticks)
                for t in SLOT_TILES[slot_no]:
                    tile = probs[:, p_at[t]:p_at[t] + width[t]]
                    pool.tensor_scalar(tile, tile, inv[:, par, stat_col[t]:stat_col[t] + 1], 1.0,
                                       ALU.mult, ALU.mult).then_inc(normed, 1)

            mul_cos_k(1)
            mul_sin(1, 1)
            mul_sin(0, 1)

            norm(0, 0, 0)
            norm(0, 0, 1)

            def head(head_no, par):
                mul_cos_k(head_no + 2)
                norm(head_no, par, 2)
                norm(head_no, par, 3)
                mul_sin(1, head_no + 2)
                mul_sin(0, head_no + 2)
                norm(head_no, par, 4)
                norm(head_no, par, 5)
                norm(head_no + 1, 1 - par, 0)
                norm(head_no + 1, 1 - par, 1)

            with pool.Fori(0, B) as b:
                wait_apart(pool, x_hi, b + 1, ticks)
                pool.tensor_tensor(kept.x_t[:, 1, :], kept.x_whole[:, :], f32(kept.x_t[:, 0, :]),
                                   ALU.subtract).then_inc(x_lo, 1)
                with pool.Fori(0, H // 2) as pair:
                    for par in range(2):
                        head(b * H + pair * 2 + par, par)

        @block.scalar
        def _(act):
            def exp(head_no, par, slot_no):
                for i, t in enumerate(SLOT_TILES[slot_no]):
                    c = stat_col[t]
                    act.wait_ge(maxed, head_no * NT + c + 1)
                    src = slot(SCORE_FILLS[slot_no], par)[:, i * BANK:i * BANK + width[t]]
                    last = act.activation(probs[:, p_at[t]:p_at[t] + width[t]], src, ACT.Exp,
                                          bias=neg_max[:, par, c:c + 1], accum_out=sums[:, par, c:c + 1])
                last.then_inc(exped, 1)

            def raw(which, fill_no, fill, par):
                act.wait_ge(filled, fill_no)
                act.activation(unrot[which][:, :], slot(fill, par), ACT.Copy).then_inc(qk_raw, 1)

            def split_hi(part, par, count):
                act.wait_ge(rotated[part], count)
                which, cols = PARTS[part]
                act.activation(qk[par][which][:, 0, cols], rot[which][:, cols], ACT.Copy).then_inc(hi_made[part], 1)

            def split_v_hi(count, fill, par, v_par):
                act.wait_ge(v_half, count)
                act.activation(v_low[v_par][:, 0, :], slot(fill, par)[:, 0:BANK], ACT.Copy).then_inc(v_hi, 1)

            def copy_turn(head_no, par, bank_no):
                act.wait_ge(turned, head_no * NB_TURN + bank_no + 1)
                for dst, src in turn_views(bank_no, par):
                    last = act.activation(dst, src, ACT.Copy)
                last.then_inc(turn_copied, 1)

            act.sem_inc(turn_copied, 2)
            act.sem_inc(y_copied, 1)
            raw(0, 1, 1, 0)
            raw(1, 2, 2, 0)
            split_v_hi(1, F_V0, 0, 0)
            split_hi(K_ALL, 0, 1)
            split_hi(Q_FIRST, 0, 1)

            split_hi(Q_REST, 0, 1)
            exp(0, 0, 0)
            exp(0, 0, 1)

            def head(head_no, par):
                nxt = 1 - par
                for part in (K_ALL, Q_FIRST, Q_REST):
                    act.wait_ge(lo_made[part], head_no + 1)
                raw(0, head_no * FILLS + F_Q, F_Q, par)
                raw(1, head_no * FILLS + F_K, F_K, par)
                copy_turn(head_no, par, 0)
                exp(head_no, par, 2)
                copy_turn(head_no, par, 1)
                copy_turn(head_no, par, 2)
                copy_turn(head_no, par, 3)
                exp(head_no, par, 3)
                split_v_hi(head_no + 2, F_V, par, nxt)
                copy_turn(head_no, par, 4)
                copy_turn(head_no, par, 5)
                copy_turn(head_no, par, 6)
                copy_turn(head_no, par, 7)
                exp(head_no, par, 4)
                split_hi(K_ALL, nxt, head_no + 2)
                exp(head_no, par, 5)
                copy_turn(head_no, par, 8)
                split_hi(Q_FIRST, nxt, head_no + 2)
                copy_turn(head_no, par, 9)
                copy_turn(head_no, par, 10)
                split_hi(Q_REST, nxt, head_no + 2)
                exp(head_no + 1, nxt, 0)
                exp(head_no + 1, nxt, 1)

            with act.Fori(0, B) as b:
                act.wait_ge(x_turned, b + 1)
                for par in range(2):
                    act.wait_ge(x_landed[par], b * (16 * H) + 32)
                for half in range(2):
                    act.activation(kept.x_whole[:, half * BANK:(half + 1) * BANK], ps_turn[:, half, :],
                                   ACT.Copy).then_inc(x_copied, 1)
                act.wait_ge(x_copied, b * 2 + 2)
                act.activation(kept.x_t[:, 0, :], kept.x_whole[:, :], ACT.Copy).then_inc(x_hi, 1)
                with act.Fori(0, H // 2) as pair:
                    for par in range(2):
                        head(b * H + pair * 2 + par, par)
                act.wait_ge(pv_done, b * H + H)
                act.wait_ge(y_free, b * 16 + 1)
                act.activation(y_out[:, :].rearrange("p (g c) -> p g c", g=2), ps_y[:, :, :],
                               ACT.Copy).then_inc(y_copied, 1)

        @block.vector
        def _(dve):

            def rowmax(head_no, par, slot_no):
                fill = SCORE_FILLS[slot_no]
                dve.wait_ge(filled, head_no * FILLS + fill)
                for i, t in enumerate(SLOT_TILES[slot_no]):
                    c = stat_col[t]
                    dve.tensor_reduce(neg_max[:, par, c:c + 1], slot(fill, par)[:, i * BANK:i * BANK + width[t]],
                                      AX.X, ALU.max, negate=True).then_inc(maxed, 1)

            def invert(head_no, par, slot_no):
                dve.wait_ge(exped, head_no * 6 + slot_no + 1)
                c = stat_col[SLOT_TILES[slot_no][0]]
                n = len(SLOT_TILES[slot_no])
                dve.reciprocal(inv[:, par, c:c + n], sums[:, par, c:c + n]).then_inc(inverted, 1)

            def mul_cos_q(count):
                dve.wait_ge(qk_raw, count * 2 - 1)
                dve.tensor_tensor(rot[0][:, :], unrot[0][:, :], kept.rope[:, 0, :], ALU.mult).then_inc(cos_made[0], 1)

            def rotate_add(part, count):
                which, cols = PARTS[part]
                dve.wait_ge(cos_made[which], count)
                dve.wait_ge(sin_made[which], count)
                dve.tensor_tensor(rot[which][:, cols], rot[which][:, cols], swapped[which][:, cols],
                                  ALU.add).then_inc(rotated[part], 1)

            def split_lo(part, par, count):
                dve.wait_ge(hi_made[part], count)
                which, cols = PARTS[part]
                dve.tensor_tensor(qk[par][which][:, 1, cols], rot[which][:, cols], f32(qk[par][which][:, 0, cols]),
                                  ALU.subtract).then_inc(lo_made[part], 1)

            def split_turn(head_no, par, bank_no):
                dve.wait_ge(turn_copied, head_no * NB_TURN + (bank_no + 3))
                for (hi, src), (lo, _) in zip(turn_views(bank_no, par, 0), turn_views(bank_no, par, 1)):
                    last = dve.tensor_tensor(lo, src, f32(hi), ALU.subtract)
                last.then_inc(turn_lo, 1)

            def first_tiles(head_no, par, first=False):
                rotate_add(Q_REST, head_no + 1)
                if not first:
                    split_turn(head_no - 1, 1 - par, 9)
                    split_turn(head_no - 1, 1 - par, 10)
                rowmax(head_no, par, 0)
                rowmax(head_no, par, 1)
                split_lo(Q_REST, par, head_no + 1)
                invert(head_no, par, 0)
                invert(head_no, par, 1)

            def split_v_lo(count, fill, par, v_par):
                dve.wait_ge(v_hi, count)
                dve.tensor_tensor(v_low[v_par][:, 1, :], slot(fill, par)[:, 0:BANK], f32(v_low[v_par][:, 0, :]),
                                  ALU.subtract).then_inc(v_lo, 1)

            def copy_v_high(fill_count, fill, par, v_par):
                dve.wait_ge(filled, fill_count)
                dve.tensor_copy(v_high[v_par][:, :], slot(fill, par)[:, BANK:T]).then_inc(v_copied, 1)

            mul_cos_q(1)
            rotate_add(K_ALL, 1)
            rotate_add(Q_FIRST, 1)
            split_v_lo(1, F_V0, 0, 0)
            copy_v_high(F_V0, F_V0, 0, 0)
            split_lo(K_ALL, 0, 1)
            split_lo(Q_FIRST, 0, 1)
            dve.sem_inc(turn_lo, 2)
            first_tiles(0, 0, True)

            def head(head_no, par):
                nxt = 1 - par
                mul_cos_q(head_no + 2)
                rowmax(head_no, par, 2)
                split_turn(head_no, par, 0)
                invert(head_no, par, 2)
                rowmax(head_no, par, 3)
                split_turn(head_no, par, 2)
                invert(head_no, par, 3)
                split_v_lo(head_no + 2, F_V, par, nxt)
                split_turn(head_no, par, 4)
                copy_v_high(head_no * FILLS + F_V, F_V, par, nxt)
                rowmax(head_no, par, 4)
                split_turn(head_no, par, 6)
                invert(head_no, par, 4)
                rotate_add(K_ALL, head_no + 2)
                rowmax(head_no, par, 5)
                split_lo(K_ALL, nxt, head_no + 2)
                invert(head_no, par, 5)
                rotate_add(Q_FIRST, head_no + 2)
                split_turn(head_no, par, 8)
                split_lo(Q_FIRST, nxt, head_no + 2)
                first_tiles(head_no + 1, nxt)

            with dve.Fori(0, B) as b:
                with dve.Fori(0, H // 2) as pair:
                    for par in range(2):
                        head(b * H + pair * 2 + par, par)

        @block.tensor
        def _(pe):
            INPUTS = [(w_in[i], x_in[i], wvo_in[i][:, :], xw_in[i]) for i in range(2)]
            FIRST = (kept.w[:, 0, :, :], kept.x_t, kept.wvo[:, 0, :], kept.x_whole)

            def project_qk(which, inputs, fill, par):
                hi, lo = ((WQ_HI, WQ_LO), (WK_HI, WK_LO))[which]
                w, xt, _, _ = inputs
                for c in range(2):
                    cols = slice(c * BANK, (c + 1) * BANK)
                    last = matmul_split(pe, slot(fill, par)[:, cols], w[:, hi, :], w[:, lo, :],
                                        xt[:, 0, cols], xt[:, 1, cols], True, True)
                last.then_inc(filled, 1)

            def project_v(inputs, fill, par, half):
                _, _, wvo, xw = inputs
                for t in range(4 * half, 4 * half + 4):
                    cols = slice(t * P, (t + 1) * P)
                    last = pe.matmul(slot(fill, par)[:, cols], xw[:, cols], wvo,
                                     start=True, stop=True)
                last.then_inc((v_half, filled)[half], 1)

            def scores(of_par, slot_no, fill, par):
                q, k = qk[of_par]
                for i, t in enumerate(SLOT_TILES[slot_no]):
                    rows = slice(t * P, (t + 1) * P)
                    for c0 in range(0, width[t], BANK):
                        n = min(BANK, width[t] - c0)
                        out = slot(fill, par)[:, i * BANK + c0:i * BANK + c0 + n]
                        pe.matmul(out, q[:, 0, rows], k[:, 0, c0:c0 + n], start=True, stop=False,
                                  skip_group_check=True)
                        if c0 + n == width[t]:
                            pe.matmul(out[:, n - P:n], ident_b[:, :], mask_b[:, :], start=False, stop=False,
                                      skip_group_check=True)
                        pe.matmul(out, q[:, 0, rows], k[:, 1, c0:c0 + n], start=False, stop=False,
                                  skip_group_check=True)
                        last = pe.matmul(out, q[:, 1, rows], k[:, 0, c0:c0 + n], start=False, stop=True,
                                         skip_group_check=True)
                last.then_inc(filled, 1)

            def turn(b, head_no, par, slot_no):
                c = max(stat_col[t] for t in SLOT_TILES[slot_no])
                pe.wait_ge(normed, head_no * NT + c + 1)
                if slot_no == 0:
                    pe.wait_ge(x_copied, b * 2 + 2)
                for bank_no, (from_slot, parts) in enumerate(TURN_BANKS):
                    if from_slot != slot_no:
                        continue
                    pe.wait_ge(turn_copied, head_no * NB_TURN + bank_no + 1)
                    if (bank_no - 2) % NB_TURN in SPLIT_BANKS:
                        splits = {0: 1, 1: 2}.get(bank_no) or 3 + SPLIT_BANKS.index(bank_no - 2)
                        pe.wait_ge(turn_lo, head_no * NB_SPLIT + splits)
                    bank, at = (bank_no + par * NB_TURN) % 2, 0
                    for t, j0, j1 in parts:
                        for j in range(j0, j1):
                            last = pe.transpose(ps_turn[:, bank, at:at + P],
                                                probs[:, p_at[t] + j * P:p_at[t] + (j + 1) * P], ident[:, :])
                            at += P
                    last.then_inc(turned, 1)

            def weigh(par, g, j_first, j_end):
                for j in range(j_first, j_end):
                    own = slice(j * P, (j + 1) * P)
                    c0 = max(0, j - 4 * g) * P
                    if j < 4:
                        probs_t = pt_split if g else pt_low
                        last = matmul_split(pe, ps_y[:, g, c0:BANK], v_low[par][:, 0, own], v_low[par][:, 1, own],
                                            probs_t[:, 0, j, c0:BANK], probs_t[:, 1, j, c0:BANK], False, False)
                    else:
                        last = pe.matmul(ps_y[:, g, c0:BANK], v_high[par][:, (j - 4) * P:(j - 3) * P], pt_high[:, j - 4, c0:BANK],
                                         start=False, stop=False, skip_group_check=True)
                return last

            def zero_y():
                for g in range(2):
                    pe.matmul(ps_y[:, g, :], zeros_b[:, 0:P], zeros_b[:, :], start=True, stop=False,
                              skip_group_check=True)

            project_qk(0, FIRST, 1, 0)
            project_qk(1, FIRST, 2, 0)
            pe.wait_ge(qk_raw, 1)
            project_v(FIRST, F_V0, 0, 0)
            project_v(FIRST, F_V0, 0, 1)
            pe.wait_ge(consts, 7)
            pe.wait_ge(lo_made[K_ALL], 1)
            pe.wait_ge(lo_made[Q_FIRST], 1)
            scores(0, 0, F_S7, 0)
            pe.wait_ge(v_lo, 1)
            pe.wait_ge(v_copied, 1)
            scores(0, 1, F_S6, 0)

            def head(b, head_no, par, inputs):
                nxt = 1 - par
                pe.wait_ge(w_landed[nxt], inputs)
                pe.wait_ge(x_landed[nxt], inputs)
                pe.wait_ge(exped, head_no * 6 + 1)
                project_qk(0, INPUTS[nxt], F_Q, par)
                pe.wait_ge(exped, head_no * 6 + 2)
                project_qk(1, INPUTS[nxt], F_K, par)
                pe.wait_ge(qk_raw, head_no * 2 + 3)
                pe.wait_ge(lo_made[Q_REST], head_no + 1)
                scores(par, 2, F_S5, par)
                turn(b, head_no, par, 0)
                pe.wait_ge(qk_raw, head_no * 2 + 4)
                scores(par, 3, F_S4, par)
                turn(b, head_no, par, 1)
                pe.wait_ge(exped, head_no * 6 + 3)
                project_v(INPUTS[nxt], F_V, par, 0)
                turn(b, head_no, par, 2)
                project_v(INPUTS[nxt], F_V, par, 1)
                pe.wait_ge(exped, head_no * 6 + 4)
                scores(par, 4, F_S10, par)
                turn(b, head_no, par, 3)
                pe.wait_ge(v_lo, head_no + 2)
                pe.wait_ge(v_copied, head_no + 2)
                scores(par, 5, F_S32, par)
                pe.wait_ge(turn_copied, head_no * NB_TURN + 2 + BANKS_HIGH)
                pe.wait_ge(turn_lo, head_no * NB_SPLIT + 4 + 2)
                weigh(par, 1, 0, 4)
                turn(b, head_no, par, 4)
                weigh(par, 1, 4, 8)
                turn(b, head_no, par, 5)
                pe.wait_ge(lo_made[K_ALL], head_no + 2)
                pe.wait_ge(lo_made[Q_FIRST], head_no + 2)
                pe.wait_ge(exped, head_no * 6 + 5)
                scores(nxt, 0, F_S7_NEXT, par)
                pe.wait_ge(exped, head_no * 6 + 6)
                scores(nxt, 1, F_S6_NEXT, par)
                pe.wait_ge(turn_copied, head_no * NB_TURN + 2 + NB_TURN)
                pe.wait_ge(turn_lo, head_no * NB_SPLIT + NB_SPLIT + 2)
                weigh(par, 0, 0, 4).then_inc(pv_done, 1)

            with pe.Fori(0, B) as b:
                pe.wait_ge(x_rows_landed, b * 16 + 16)
                pe.wait_ge(turn_copied, b * (H * NB_TURN) + 2)
                pe.wait_ge(turn_lo, b * (H * NB_SPLIT) + 2)
                for t in range(NT):
                    last = pe.transpose(ps_turn[:, t // 4, t % 4 * P:(t % 4 + 1) * P], kept.x_rows[:, t, :],
                                        ident[:, :])
                last.then_inc(x_turned, 1)
                pe.wait_ge(y_copied, b + 1)
                zero_y()
                with pe.Fori(0, H // 2) as pair:
                    heads = b * H + pair * 2
                    loads = b * (H // 2) + pair
                    head(b, heads, 0, loads * 32 + 32)
                    head(b, heads + 1, 1, loads * 32 + 64)


ROW_TILES = ((0,), (1,), (2,), (3,), (4, 5), (6, 7), (8, 9), (10, 11))
FFN_FILLS = 12
F_D0, F_D1, F_D2, F_D3, F_TOKENS, F_C0, F_C1, F_C2, F_C3, F_H01, F_H23, F_ZT = range(1, 13)
F_ROWS = (F_D0, F_D1, F_D2, F_D3, F_C0, F_C1, F_C2, F_C3)


def ffn_block(nc, x, y_t, gamma_x, gamma_slot, slots, w1, w2, out):
    B, T, D = x.shape
    N = slots.shape[0] * slots.shape[1]
    F = w1.shape[1]
    NT, NC, FC = T // P, N // P, F // P
    assert D == P and N == BANK and F == BANK and NT == 8 and B % 2 == 0 and B >= 4

    with ExitStack() as ctx:
        s = Scope(nc, ctx)
        y_in = s.sb("y_in", [P, T], F32)
        x_row = s.sb("x_row1", [P, NT, D], F32)
        res = s.sb("res", [P, NT, D], F32)
        x1 = [s.sb(f"x1_{i}", [P, NT, D], F32) for i in range(2)]
        z_row = [s.sb(f"z_row{i}", [P, NT, D], F32) for i in range(2)]
        z_t = s.sb("z_t", [P, 2, T], F32R)
        rows_n = s.sb("rows_n", [P, 4, T], F32)
        rows_s = s.sb("rows_s", [P, 4, N], F32)
        disp = s.sb("disp", [P, NT, N], F32)
        comb = s.sb("comb", [P, 2, NC, T], F32R)
        slot_in = s.sb("slot_in", [P, 2, N], F32R)
        hid = s.sb("hid", [P, FC, N], F32)
        proc = s.sb("proc", [P, 2, NC * D], F32R)
        o_t = s.sb("o_t", [P, T], F32)
        res2 = s.sb("res2", [P, NT, D], F32)
        out_row = s.sb("out_row", [P, NT, D], F32)
        stats = s.sb("stats", [P, 2, NT, 6], F32)
        mv = s.sb("mv", [P, 2, NT, 2], F32)
        neg_mean = s.sb("neg_mean", [P, 2, NT], F32)
        rstd = s.sb("rstd", [P, 2, NT], F32)
        power = s.sb("power", [P, 2, NT], F32)
        rms = s.sb("rms", [P, NT], F32)
        z_scale = s.sb("z_scale", [P, NT], F32)
        minus_half = s.sb("minus_half", [P, NT], F32)
        neg_max = s.sb("neg_max1", [P, 4 + NT], F32)
        sums = s.sb("sums1", [P, 4 + NT], F32)
        inv = s.sb("inv1", [P, 4 + NT], F32)
        ident = s.sb("ident2", [P, P], F32)
        gammas = s.sb("gammas", [P, 2], F32)
        gamma_both = s.sb("gamma_both", [P, 1], F32)
        w1_raw = s.sb("w1_raw", [P, F], F32)
        w2_in = s.sb("w2_in", [P, FC, D], F32)
        w1_s = s.sb("w1_s", [P, 2, F], F32R)
        se_raw = s.sb("se_raw", [P, NC, D], F32)
        se_sq = s.sb("se_sq", [P, NC, D], F32)
        se_row = s.sb("se_row", [P, NC, D], F32)
        se_t = s.sb("se_t", [P, 2, N], F32R)
        ps_slot = s.ps("ps_slot1", [P, 2, T])
        ps_turn = s.ps("ps_turn1", [P, 2, BANK])
        ps_acc = s.ps("ps_acc", [P, 2, BANK])

        w_landed, in_landed = s.sem("w_landed1"), s.sem("in_landed_f")
        consts, setup, se_norm = s.sem("consts1"), s.sem("setup"), s.sem("se_norm")
        ticks, dve_ticks = s.sem("ticks1"), s.sem("dve_ticks")
        filled, turned = s.sem("filled1"), s.sem("turned1")
        slots_summed, proc_summed = s.sem("slots_summed"), s.sem("proc_summed")
        out_summed, out_turned = s.sem("out_summed"), s.sem("out_turned")
        maxed, inverted = s.sem("maxed1"), s.sem("inverted1")
        added1, added2 = s.sem("added1"), s.sem("added2")
        stats_a, stats_b = s.sem("stats_a"), s.sem("stats_b")
        z_made, x1_made = s.sem("z_made"), s.sem("x1_made")
        stats2_a, stats2_b = s.sem("stats2_a"), s.sem("stats2_b")
        disp_dve, turn_lo, zt_lo = s.sem("disp_dve"), s.sem("turn_lo1"), s.sem("zt_lo")
        slot_in_hi, slot_in_lo, proc_lo = s.sem("slot_in_hi"), s.sem("slot_in_lo"), s.sem("proc_lo")
        exped, disp_act, turn_hi = s.sem("exped1"), s.sem("disp_act"), s.sem("turn_hi1")
        zt_hi, gelued = s.sem("zt_hi"), s.sem("gelued")
        proc_hi, o_copied = s.sem("proc_hi"), s.sem("o_copied")
        normed = s.sem("normed1")
        ln_step, norm1_known = s.sem("ln_step"), s.sem("norm1_known")
        out_made, out_free = s.sem("out_made"), s.sem("out_free")

        def slot(fill):
            return ps_slot[:, (fill - 1) % 2, :]

        def count(b, fill):
            return b * FFN_FILLS + (2 + fill)

        def row_tile(i, k):
            src = slot(F_ROWS[k])
            if i < 4:
                return src, rows_n[:, i, :]
            return src[:, (i % 2) * BANK:(i % 2 + 1) * BANK], rows_s[:, i % 4, :]

        def disp_view(bank_no):
            c, half = bank_no // 2, bank_no % 2
            return disp[:, 4 * half:4 * half + 4, c * P:(c + 1) * P]

        def comb_view(bank_no, part):
            t = bank_no - 8
            return comb[:, part, :, t * P:(t + 1) * P]

        def turn_src(bank_no):
            return ps_turn[:, bank_no % 2, :].rearrange("p (j c) -> p j c", c=P)

        block = ctx.enter_context(nc.Block())

        @block.sync
        def _(sp):
            def load(b):
                sp.dma_start(y_in[:, :], y_t[b, :, :]).then_inc(in_landed, 16)
                sp.dma_start(x_row[:, :, :], x[b, :, :].rearrange("(t p) m -> p t m", p=P)).then_inc(in_landed, 16)

            def store(b):
                sp.wait_ge(out_made, b * NT + (NT + 1))
                sp.dma_start(out[b, :, :].rearrange("(t p) m -> p t m", p=P), out_row[:, :, :])\
                  .then_inc(out_free, 16)

            load(0)
            sp.dma_start(gammas[:, 0:1], gamma_x.rearrange("(p a) -> p a", a=1)).then_inc(w_landed, 16)
            sp.dma_start(gammas[:, 1:2], gamma_slot.rearrange("(p a) -> p a", a=1)).then_inc(w_landed, 16)
            sp.dma_start(se_raw[:, :, :], slots.rearrange("e t d -> (e t) d").rearrange("(c p) d -> p c d", p=P))\
              .then_inc(w_landed, 16)
            sp.dma_start(w1_raw[:, :], w1).then_inc(w_landed, 16)
            sp.dma_start(w2_in[:, :, :], w2.rearrange("(c p) d -> p c d", p=P)).then_inc(w_landed, 16)
            for b in (1, 2):
                sp.wait_ge(added1, b)
                load(b)
            with sp.Fori(1, B - 2) as b:
                sp.wait_ge(added1, b + 2)
                load(b + 2)
                store(b - 1)
            for b in range(B - 3, B):
                store(b)
            sp.wait_ge(out_free, 16 * B + 1)

        @block.gpsimd
        def _(pool):
            pool.memset(ident[:, :], 0.0).then_inc(consts, 1)
            pool.memset(minus_half[:, :], -0.5).then_inc(consts, 1)
            pool.memset(out_row[:, :, :], 0.0).then_inc(out_free, 1)
            pool.sem_inc(out_made, 1)
            pool.wait_ge(consts, 2)
            pool.affine_select(out=ident[:, :], in_=ident[:, :], compare_op=ALU.not_equal, fill=1.0,
                               base=0, pattern=[[-1, P]], channel_multiplier=1).then_inc(consts, 1)

            class Steps:
                at = 0

            def step(ins, base):
                Steps.at += 1
                ins.then_inc(ln_step, 1)
                wait_apart(pool, ln_step, base + Steps.at, ticks)

            def mean_rstd(which, base):
                step(pool.tensor_scalar(neg_mean[:, which, :], mv[:, which, :, 0], -1.0, 1.0, ALU.mult, ALU.mult), base)
                step(pool.tensor_scalar(power[:, which, :], mv[:, which, :, 1], LN_EPS, 1.0, ALU.add, ALU.mult), base)
                step(pool.tensor_tensor(rstd[:, which, :], power[:, which, :], minus_half[:, :], ALU.pow), base)

            def first_norm(stats_count, base):
                wait_apart(pool, stats_b, stats_count, ticks)
                mean_rstd(0, base)
                step(pool.tensor_tensor(rms[:, :], mv[:, 0, :, 1], rstd[:, 0, :], ALU.mult), base)
                step(pool.tensor_tensor(rms[:, :], rms[:, :], rstd[:, 0, :], ALU.mult), base)
                step(pool.tensor_scalar(rms[:, :], rms[:, :], 1e-24 / D, 1.0, ALU.max, ALU.mult), base)
                step(pool.tensor_tensor(rms[:, :], rms[:, :], minus_half[:, :], ALU.pow), base)
                pool.tensor_tensor(z_scale[:, :], rms[:, :], rstd[:, 0, :], ALU.mult).then_inc(norm1_known, 1)

            def second_norm(b, base):
                wait_apart(pool, stats2_b, b + 1, ticks)
                mean_rstd(1, base)

            def output_rows(b):
                wait_apart(pool, out_free, b * 16 + 1, ticks)
                for t in range(NT):
                    pool.tensor_scalar(out_row[:, t, :], res2[:, t, :], neg_mean[:, 1, t:t + 1],
                                       rstd[:, 1, t:t + 1], ALU.add, ALU.mult).then_inc(out_made, 1)

            def norm_rows(b, i):
                wait_apart(pool, inverted, b * 12 + i + 1, ticks)
                _, row = row_tile(i, 0)
                pool.tensor_scalar(row, row, inv[:, i:i + 1], 1.0, ALU.mult, ALU.mult).then_inc(normed, 1)

            pool.wait_ge(setup, NC)
            step(pool.tensor_scalar(rms[:, 0:NC], rms[:, 0:NC], 1e-24, 1.0, ALU.max, ALU.mult), 0)
            step(pool.tensor_tensor(rms[:, 0:NC], rms[:, 0:NC], minus_half[:, 0:NC], ALU.pow), 0)
            for c in range(NC):
                last = pool.tensor_scalar(se_row[:, c, :], se_raw[:, c, :], rms[:, c:c + 1], float(D) ** 0.5,
                                          ALU.mult, ALU.mult)
            last.then_inc(se_norm, 1)
            pool.wait_ge(se_norm, 1)
            first_norm(1, 0)
            ahead_of_one, per_batch = Steps.at + 7, 7 + 3

            def batch(b, par, first, ahead):
                base = 0 if first else (b - 1) * per_batch
                if not first:
                    Steps.at = ahead_of_one
                for i in range(8):
                    norm_rows(b, i)
                if ahead:
                    first_norm(b + 2, base)
                for i in range(8, 10):
                    norm_rows(b, i)
                if not first:
                    second_norm(b - 1, base)
                for i in range(10, 12):
                    norm_rows(b, i)
                if not first:
                    output_rows(b - 1)

            batch(0, 0, True, True)
            with pool.Fori(0, B // 2 - 1) as pair:
                batch(pair * 2 + 1, 1, False, True)
                batch(pair * 2 + 2, 0, False, True)
            batch(B - 1, 1, False, False)
            second_norm(B - 1, (B - 2) * per_batch)
            output_rows(B - 1)

        @block.scalar
        def _(act):
            def exp(b, k):
                for i in ROW_TILES[k]:
                    act.wait_ge(maxed, b * 12 + i + 1)
                    src, row = row_tile(i, k)
                    last = act.activation(row, src, ACT.Exp, bias=neg_max[:, i:i + 1], accum_out=sums[:, i:i + 1])
                last.then_inc(exped, 1)

            def wait_turned(b, bank_no):
                act.wait_ge(turned, b * 16 + (bank_no + 2))

            def copy_disp(b, bank_no):
                wait_turned(b, bank_no)
                act.activation(disp_view(bank_no), turn_src(bank_no), ACT.Copy).then_inc(disp_act, 1)

            def split_comb(b, step):
                for bank_no in (2 * step, 2 * step + 1):
                    wait_turned(b, bank_no)
                    act.activation(comb_view(bank_no, 0), turn_src(bank_no), ACT.Copy).then_inc(turn_hi, 1)

            def split_zt(fill_count, fill):
                act.wait_ge(filled, fill_count)
                act.activation(z_t[:, 0, :], slot(fill), ACT.Copy).then_inc(zt_hi, 1)

            def split_proc(b):
                act.wait_ge(proc_summed, b + 1)
                act.activation(proc[:, 0, :], ps_acc[:, 1, :], ACT.Copy).then_inc(proc_hi, 1)

            def copy_out(b, half):
                act.wait_ge(out_summed, b * 2 + (half + 1))
                act.activation(o_t[:, half * BANK:(half + 1) * BANK], ps_acc[:, half, :], ACT.Copy).then_inc(o_copied, 1)

            def gelu(b, fill, half):
                act.wait_ge(filled, count(b, fill))
                for i in range(2):
                    act.activation(hid[:, 2 * half + i, :], slot(fill)[:, i * BANK:(i + 1) * BANK],
                                   ACT.Gelu).then_inc(gelued, 1)

            split_zt(2, F_ZT)

            def batch(b, first, ahead):
                if not first:
                    split_proc(b - 1)
                exp(b, 0)
                exp(b, 1)
                if not first:
                    copy_out(b - 1, 0)
                copy_disp(b, 0)
                copy_disp(b, 2)
                exp(b, 2)
                exp(b, 3)
                if not first:
                    copy_out(b - 1, 1)
                copy_disp(b, 4)
                copy_disp(b, 6)
                exp(b, 4)
                exp(b, 5)
                split_comb(b, 4)
                exp(b, 6)
                split_comb(b, 5)
                exp(b, 7)
                gelu(b, F_H01, 0)
                split_comb(b, 6)
                gelu(b, F_H23, 1)
                split_comb(b, 7)
                if ahead:
                    split_zt(count(b, F_ZT), F_ZT)

            batch(0, True, True)
            with act.Fori(1, B - 1) as b:
                batch(b, False, True)
            batch(B - 1, False, False)
            split_proc(B - 1)
            copy_out(B - 1, 0)
            copy_out(B - 1, 1)

        @block.vector
        def _(dve):
            dve.wait_ge(w_landed, 80)
            for c in range(NC):
                dve.tensor_tensor_reduce(se_sq[:, c, :], se_raw[:, c, :], se_raw[:, c, :], 1.0, 0.0,
                                         ALU.mult, ALU.add, rms[:, c:c + 1]).then_inc(setup, 1)
            dve.tensor_tensor(gamma_both[:, :], gammas[:, 0:1], gammas[:, 1:2], ALU.mult).then_inc(setup, 1)
            dve.tensor_copy(w1_s[:, 0, :], w1_raw[:, :]).then_inc(setup, 1)

            def add1(fill_count, fill, adds):
                dve.wait_ge(in_landed, adds * 32)
                dve.wait_ge(filled, fill_count)
                dve.tensor_tensor(res[:, :, :], slot(fill).rearrange("p (t m) -> p t m", m=D), x_row[:, :, :],
                                  ALU.add).then_inc(added1, 1)

            def add2(par, adds):
                dve.wait_ge(out_turned, adds)
                dve.wait_ge(x1_made, adds * 2)
                dve.wait_ge(out_made, (adds - 1) * NT + 1)
                dve.tensor_tensor(res2[:, :, :], ps_acc[:, :, :].rearrange("p h (t m) -> p (h t) m", m=D),
                                  x1[par][:, :, :], ALU.add).then_inc(added2, 1)

            def row_stats(which, adds):
                src, added, tiles_done, done = ((res, added1, stats_a, stats_b), (res2, added2, stats2_a, stats2_b))[which]
                dve.wait_ge(added, adds)
                for t in range(NT):
                    last = dve.bn_stats(stats[:, which, t, :], src[:, t, :])
                last.then_inc(tiles_done, 1)
                wait_apart(dve, tiles_done, adds, dve_ticks)
                for t in range(NT):
                    last = dve.bn_aggr(mv[:, which, t, :], stats[:, which, t, :])
                last.then_inc(done, 1)

            def z_rows(par, adds):
                dve.wait_ge(norm1_known, adds)
                for t in range(NT):
                    last = dve.tensor_scalar(z_row[par][:, t, :], res[:, t, :], neg_mean[:, 0, t:t + 1],
                                             z_scale[:, t:t + 1], ALU.add, ALU.mult)
                last.then_inc(z_made, 1)

            def x1_rows(par, tiles):
                for t in tiles:
                    last = dve.tensor_scalar(x1[par][:, t, :], res[:, t, :], neg_mean[:, 0, t:t + 1],
                                             rstd[:, 0, t:t + 1], ALU.add, ALU.mult)
                last.then_inc(x1_made, 1)

            def split_zt(splits, fill):
                dve.wait_ge(zt_hi, splits)
                dve.tensor_tensor(z_t[:, 1, :], slot(fill), f32(z_t[:, 0, :]), ALU.subtract).then_inc(zt_lo, 1)

            def rowmax(b, k):
                dve.wait_ge(filled, count(b, F_ROWS[k]))
                for i in ROW_TILES[k]:
                    src, _ = row_tile(i, k)
                    dve.tensor_reduce(neg_max[:, i:i + 1], src, AX.X, ALU.max, negate=True).then_inc(maxed, 1)

            def invert(b, k):
                dve.wait_ge(exped, b * 8 + (k + 1))
                i, n = ROW_TILES[k][0], len(ROW_TILES[k])
                dve.reciprocal(inv[:, i:i + n], sums[:, i:i + n]).then_inc(inverted, n)

            def copy_disp(b, bank_no):
                dve.wait_ge(turned, b * 16 + (bank_no + 2))
                dve.tensor_copy(disp_view(bank_no), turn_src(bank_no)).then_inc(disp_dve, 1)

            def split_comb(b, step):
                for bank_no in (2 * step, 2 * step + 1):
                    dve.wait_ge(turn_hi, b * 8 + (bank_no - 8 + 1))
                    dve.tensor_tensor(comb_view(bank_no, 1), turn_src(bank_no), f32(comb_view(bank_no, 0)),
                                      ALU.subtract).then_inc(turn_lo, 1)

            def split_slot_in(b):
                dve.wait_ge(slots_summed, b + 1)
                dve.tensor_scalar(slot_in[:, 0, :], ps_acc[:, 0, :], gammas[:, 0:1], None,
                                  ALU.mult).then_inc(slot_in_hi, 1)
                dve.wait_ge(slot_in_hi, b + 1)
                dve.scalar_tensor_tensor(slot_in[:, 1, :], ps_acc[:, 0, :], gammas[:, 0:1],
                                         f32(slot_in[:, 0, :]), ALU.mult, ALU.subtract).then_inc(slot_in_lo, 1)

            def split_proc(b):
                dve.wait_ge(proc_hi, b + 1)
                dve.tensor_tensor(proc[:, 1, :], ps_acc[:, 1, :], f32(proc[:, 0, :]), ALU.subtract).then_inc(proc_lo, 1)

            add1(1, F_TOKENS, 1)
            row_stats(0, 1)
            dve.wait_ge(setup, NC + 2)
            dve.tensor_tensor(w1_s[:, 1, :], w1_raw[:, :], f32(w1_s[:, 0, :]), ALU.subtract).then_inc(setup, 1)
            dve.wait_ge(turned, 1)
            dve.tensor_scalar(se_t[:, 0, :], ps_turn[:, 0, :], gamma_both[:, 0:1], None, ALU.mult).then_inc(setup, 1)
            dve.wait_ge(setup, NC + 4)
            dve.scalar_tensor_tensor(se_t[:, 1, :], ps_turn[:, 0, :], gamma_both[:, 0:1], f32(se_t[:, 0, :]),
                                     ALU.mult, ALU.subtract).then_inc(turn_lo, 1)
            dve.memset(neg_max[:, :], 0.0).then_inc(turn_lo, 1)
            dve.wait_ge(turn_lo, 2)
            z_rows(0, 1)
            split_zt(1, F_ZT)

            def batch(b, par, first, ahead):
                if not first:
                    split_proc(b - 1)
                rowmax(b, 0)
                rowmax(b, 1)
                invert(b, 0)
                x1_rows(par, range(NT // 2))
                invert(b, 1)
                x1_rows(par, range(NT // 2, NT))
                copy_disp(b, 1)
                rowmax(b, 2)
                copy_disp(b, 3)
                invert(b, 2)
                rowmax(b, 3)
                invert(b, 3)
                copy_disp(b, 5)
                if not first:
                    add2(1 - par, b)
                if ahead:
                    add1(count(b, F_TOKENS), F_TOKENS, b + 2)
                copy_disp(b, 7)
                rowmax(b, 4)
                rowmax(b, 5)
                invert(b, 4)
                if ahead:
                    row_stats(0, b + 2)
                invert(b, 5)
                if not first:
                    row_stats(1, b)
                split_comb(b, 4)
                rowmax(b, 6)
                invert(b, 6)
                split_slot_in(b)
                rowmax(b, 7)
                split_comb(b, 5)
                invert(b, 7)
                if ahead:
                    z_rows(1 - par, b + 2)
                split_comb(b, 6)
                split_comb(b, 7)
                if ahead:
                    split_zt(b + 2, F_ZT)

            batch(0, 0, True, True)
            with dve.Fori(0, B // 2 - 1) as pair:
                batch(pair * 2 + 1, 1, False, True)
                batch(pair * 2 + 2, 0, False, True)
            batch(B - 1, 1, False, False)
            split_proc(B - 1)
            add2(1, B)
            row_stats(1, B)

        @block.tensor
        def _(pe):
            pe.wait_ge(consts, 3)

            def transposes(dst, src, done):
                for t in range(NT):
                    last = pe.transpose(dst(t), src[:, t * P:(t + 1) * P], ident[:, :])
                last.then_inc(done, 1)

            def in_slot(fill):
                return lambda t: slot(fill)[:, t * P:(t + 1) * P]

            def rows(k):
                for i in ROW_TILES[k]:
                    dst, _ = row_tile(i, k)
                    if i < 4:
                        own = slice(i * P, (i + 1) * P)
                        for c in range(2):
                            cols = slice(c * BANK, (c + 1) * BANK)
                            last = matmul_split(pe, dst[:, cols], se_t[:, 0, own], se_t[:, 1, own],
                                                z_t[:, 0, cols], z_t[:, 1, cols], True, True)
                    else:
                        own = slice((i - 4) * P, (i - 3) * P)
                        last = matmul_split(pe, dst, z_t[:, 0, own], z_t[:, 1, own],
                                            se_t[:, 0, :], se_t[:, 1, :], True, True)
                last.then_inc(filled, 1)

            def turn(b, k):
                for bank_no in (2 * k, 2 * k + 1):
                    i, blocks = (k, bank_no % 2 * 4) if k < 4 else (bank_no - 4, 0)
                    pe.wait_ge(normed, b * 12 + (i + 1))
                    if bank_no < 2:
                        pe.wait_ge(turn_lo, b * 8 + (bank_no + 1))
                    elif bank_no < 10:
                        pe.wait_ge((disp_act, disp_dve)[bank_no % 2], b * 4 + bank_no // 2)
                    else:
                        pe.wait_ge(turn_lo, b * 8 + (bank_no - 10 + 3))
                    _, row = row_tile(i, k)
                    for j in range(4):
                        last = pe.transpose(ps_turn[:, bank_no % 2, j * P:(j + 1) * P],
                                            row[:, (blocks + j) * P:(blocks + j + 1) * P], ident[:, :])
                    last.then_inc(turned, 1)

            def sum_slots(par, tiles):
                for t in tiles:
                    last = pe.matmul(ps_acc[:, 0, :], z_row[par][:, t, :], disp[:, t, :],
                                     start=t == 0, stop=t == NT - 1, skip_group_check=True)
                return last

            def sum_out(half):
                cols = slice(half * BANK, (half + 1) * BANK)
                for c in range(NC):
                    own = slice(c * P, (c + 1) * P)
                    last = matmul_split(pe, ps_acc[:, half, :], proc[:, 0, own], proc[:, 1, own],
                                        comb[:, 0, c, cols], comb[:, 1, c, cols], c == 0, c == NC - 1)
                last.then_inc(out_summed, 1)

            def out_half(b, half):
                if half == 0:
                    pe.wait_ge(proc_lo, b + 1)
                    pe.wait_ge(turn_lo, b * 8 + 10)
                sum_out(half)

            def turn_out(b):
                pe.wait_ge(o_copied, b * 2 + 2)
                transposes(lambda t: ps_acc[:, t // 4, t % 4 * P:(t % 4 + 1) * P], o_t, out_turned)

            def hidden(fill, half):
                for i in range(2):
                    own = slice((2 * half + i) * P, (2 * half + i + 1) * P)
                    last = matmul_split(pe, slot(fill)[:, i * BANK:(i + 1) * BANK], w1_s[:, 0, own], w1_s[:, 1, own],
                                        slot_in[:, 0, :], slot_in[:, 1, :], True, True)
                last.then_inc(filled, 1)

            def z_transposes(par, fill):
                rows_of_z = z_row[par][:, :, :].rearrange("p t m -> p (t m)")
                transposes(in_slot(fill), rows_of_z, filled)

            pe.wait_ge(in_landed, 32)
            transposes(in_slot(F_TOKENS), y_in, filled)
            pe.wait_ge(se_norm, 1)
            for c in range(NC):
                last = pe.transpose(ps_turn[:, 0, c * P:(c + 1) * P], se_row[:, c, :], ident[:, :])
            last.then_inc(turned, 1)
            pe.wait_ge(z_made, 1)
            z_transposes(0, F_ZT)

            def batch(b, par, first, ahead):
                pe.wait_ge(zt_lo, b + 1)
                if first:
                    pe.wait_ge(turn_lo, 2)
                    pe.wait_ge(added1, 1)
                rows(0)
                if not first:
                    pe.wait_ge(gelued, b * FC)
                rows(1)
                if not first:
                    out_half(b - 1, 0)
                turn(b, 0)
                pe.wait_ge(exped, b * 8 + 1)
                rows(2)
                turn(b, 1)
                pe.wait_ge(exped, b * 8 + 2)
                rows(3)
                if not first:
                    out_half(b - 1, 1)
                turn(b, 2)
                if not first:
                    turn_out(b - 1)
                pe.wait_ge(exped, b * 8 + 3)
                if ahead:
                    pe.wait_ge(in_landed, b * 32 + 64)
                    transposes(in_slot(F_TOKENS), y_in, filled)
                else:
                    pe.sem_inc(filled, 1)
                turn(b, 3)
                pe.wait_ge(exped, b * 8 + 4)
                rows(4)
                if ahead:
                    pe.wait_ge(added1, b + 2)
                rows(5)
                pe.wait_ge(disp_act, b * 4 + 4)
                pe.wait_ge(disp_dve, b * 4 + 4)
                if not first:
                    pe.wait_ge(added2, b)
                sum_slots(par, range(NT // 2))
                turn(b, 4)
                pe.wait_ge(exped, b * 8 + 5)
                rows(6)
                sum_slots(par, range(NT // 2, NT)).then_inc(slots_summed, 1)
                turn(b, 5)
                pe.wait_ge(exped, b * 8 + 6)
                rows(7)
                pe.wait_ge(slot_in_lo, b + 1)
                pe.wait_ge(exped, b * 8 + 7)
                hidden(F_H01, 0)
                turn(b, 6)
                pe.wait_ge(exped, b * 8 + 8)
                hidden(F_H23, 1)
                turn(b, 7)
                if ahead:
                    pe.wait_ge(gelued, b * FC + 2)
                    pe.wait_ge(z_made, b + 2)
                    z_transposes(1 - par, F_ZT)
                pe.wait_ge(gelued, b * FC + FC)
                for n in range(NC):
                    own = slice(n * P, (n + 1) * P)
                    for c in range(FC):
                        last = pe.matmul(ps_acc[:, 1, own], hid[:, c, own], w2_in[:, c, :],
                                         start=c == 0, stop=c == FC - 1)
                last.then_inc(proc_summed, 1)

            batch(0, 0, True, True)
            with pe.Fori(0, B // 2 - 1) as pair:
                batch(pair * 2 + 1, 1, False, True)
                batch(pair * 2 + 2, 0, False, True)
            batch(B - 1, 1, False, False)
            out_half(B - 1, 0)
            out_half(B - 1, 1)
            turn_out(B - 1)


def build(nc, x, wq, wk, wv, wo, gamma_x, gamma_slot, slots, w1, w2, rope_c, rope_s, out):
    B, T, M = x.shape
    H = wq.shape[1]
    y_t = nc.dram_tensor("y_t", (B, M, T), F32, kind="Internal").ap()
    with ExitStack() as ctx:
        kept = Kept(Scope(nc, ctx), H, T)
        prepare_block(nc, x, wq, wk, wv, wo, rope_c, rope_s, kept)
        attention_block(nc, x, kept, y_t, B, H, T)
    ffn_block(nc, x, y_t, gamma_x, gamma_slot, slots, w1, w2, out)


_INS = ["L0_attn_x", "L0_attn_wq", "L0_attn_wk", "L0_attn_wv", "L0_attn_wo", "L0_ffn_gamma_x",
        "L0_ffn_gamma_slot", "L0_ffn_slot_embeds", "L0_ffn_w1", "L0_ffn_w2"]


def kernel(**inputs):
    import concourse.bacc as _bacc
    from concourse.bass_utils import run_bass_kernel_spmd as _run

    nc = _bacc.Bacc("TRN2", target_bir_lowering=False, num_devices=1)
    arrays = {f"in_{name}": np.ascontiguousarray(inputs[name]) for name in _INS}
    shape = arrays["in_L0_attn_x"].shape
    arrays["rope_c"], arrays["rope_s"] = rope_tables(shape[1], inputs["L0_attn_wq"].shape[2])
    args = [nc.dram_tensor(n, a.shape, mybir.dt.from_np(a.dtype), kind="ExternalInput").ap()
            for n, a in arrays.items()]
    out = nc.dram_tensor("out_0", shape, F32, kind="ExternalOutput").ap()
    build(nc, *args, out)
    r = _run(nc, [arrays], core_ids=[0])
    return r.results[0]["out_0"]
```
